# Optimizing a Trainium2 kernel written in Bass

```python
import numpy as np
import jax
import jax.numpy as jnp

def _softmax(x, axis=-1):
    return jax.nn.softmax(x, axis=axis)

def _gelu(x):
    return jax.nn.gelu(x, approximate=True)

def _silu(x):
    return jax.nn.silu(x)

def _sigmoid(x):
    return jax.nn.sigmoid(x)

def _layernorm(x, axis=-1, eps=1e-05):
    m = jnp.mean(x, axis=axis, keepdims=True)
    v = jnp.var(x, axis=axis, keepdims=True)
    return (x - m) / jnp.sqrt(v + eps)

def _scatter_add(tgt, idx, src, axis=0):
    return tgt.at[idx].add(src)

def _segment_sum(src, seg, n):
    return jax.ops.segment_sum(src, seg, n)
kernel_name = 'mk_adj_resnorm_d1_adj_r2_348090'

def setup_inputs(seed: int=0):
    np.random.seed(seed)
    _w = jnp.asarray

    def _rec_inputs():
        import jax
        import jax.numpy as jnp
        _gk = jax.random.key(seed)
        x = -9.806e-05 + 1 * jax.random.normal(jax.random.fold_in(_gk, 1), (8192, 128), jnp.float32)
        _w = (1.0 + jnp.arange(8192, dtype=jnp.float32)) ** (-0.5)
        _w = _w / _w.mean()
        _pij = jnp.clip(0.00195312 * _w[:, None] * _w[None, :], 0.0, 1.0)
        _a = jax.random.uniform(jax.random.fold_in(_gk, 2), (8192, 8192)) < _pij
        _a = jnp.logical_or(_a, jnp.eye(8192, dtype=bool))
        _af = _a.astype(jnp.float32)
        adj = _af
        return (x, adj)
    x, adj = _rec_inputs()

    def _L0_gnn_setup():
        import jax, jax.numpy as jnp
        import numpy as np
        N, F_IN, HEADS, F_OUT = (2048, 128, 4, 32)
        DENSITY = 0.05
        key = jax.random.key(seed)
        k_x, k_adj, k_w, k_as, k_ad, k_b = jax.random.split(key, 6)
        x = jax.random.normal(k_x, (N, F_IN), dtype=jnp.float32)
        adj = (jax.random.uniform(k_adj, (N, N)) < DENSITY).astype(jnp.float32)
        adj = jnp.maximum(adj, jnp.eye(N, dtype=jnp.float32))
        weight = jax.random.normal(k_w, (HEADS * F_OUT, F_IN), dtype=jnp.float32) * 0.1
        att_src = jax.random.normal(k_as, (1, HEADS, F_OUT), dtype=jnp.float32) * 0.1
        att_dst = jax.random.normal(k_ad, (1, HEADS, F_OUT), dtype=jnp.float32) * 0.1
        bias = jax.random.normal(k_b, (HEADS * F_OUT,), dtype=jnp.float32) * 0.1
        return {'x': x, 'adj_matrix': adj, 'weight': weight, 'att_src': att_src, 'att_dst': att_dst, 'bias': bias}
    _L0_gnn_all = _L0_gnn_setup()
    _L0_gnn_in = {k: v for k, v in _L0_gnn_all.items() if k in ('weight', 'att_src', 'att_dst', 'bias')}
    del _L0_gnn_all
    return {'x': x, 'adj': adj, 'L0_gnn_weight': _L0_gnn_in['weight'], 'L0_gnn_att_src': _L0_gnn_in['att_src'], 'L0_gnn_att_dst': _L0_gnn_in['att_dst'], 'L0_gnn_bias': _L0_gnn_in['bias']}

def reference(x, adj, L0_gnn_weight, L0_gnn_att_src, L0_gnn_att_dst, L0_gnn_bias):
    import jax
    import jax.numpy as jnp

    def _L0_gnn_ref(x, adj_matrix, weight, att_src, att_dst, bias):
        import jax, jax.numpy as jnp
        import numpy as np
        N, F_IN, HEADS, F_OUT = (2048, 128, 4, 32)
        DENSITY = 0.05
        n = x.shape[0]
        heads = att_src.shape[1]
        f_out = weight.shape[0] // heads
        h_prime = (x @ weight.T).reshape(n, heads, f_out)
        alpha_src = jnp.sum(h_prime * att_src, axis=-1)
        alpha_dst = jnp.sum(h_prime * att_dst, axis=-1)
        C = alpha_src[None, :, :] + alpha_dst[:, None, :]
        adj_t = adj_matrix.T[..., None]
        tau = adj_t * jnp.exp(jnp.maximum(0.2 * C, C))
        tau_sum = jnp.sum(tau, axis=1, keepdims=True)
        att_weights = tau / tau_sum
        z = jnp.einsum('mnh,nhf->mhf', adj_t * att_weights, h_prime)
        return z.reshape(n, heads * f_out) + bias
    x = _layernorm(x + _L0_gnn_ref(x, adj, L0_gnn_weight, L0_gnn_att_src, L0_gnn_att_dst, L0_gnn_bias), axis=-1)
    return x

_drawn_inputs = setup_inputs


def setup_inputs(seed=0):
    import zlib

    import numpy as np

    out = dict(_drawn_inputs(seed))
    spreads = {}
    factors = {}
    for name, (base, spread) in spreads.items():
        noise = np.random.default_rng([zlib.crc32(name.encode()), seed]).standard_normal(out[name].shape)
        drawn = base * np.exp(spread * noise) if base else spread * noise
        out[name] = jnp.asarray(drawn.astype(out[name].dtype))
    for name, factor in factors.items():
        out[name] = (out[name] * factor).astype(out[name].dtype)
    return out
```

```python
from contextlib import ExitStack

import concourse.bass as bass
from concourse import mybir

ALU = mybir.AluOpType
ACT = mybir.ActivationFunctionType
AX = mybir.AxisListType
F32 = mybir.dt.float32
F16 = mybir.dt.float16
F8 = mybir.dt.float8e4
U8 = mybir.dt.uint8
I32 = mybir.dt.int32

P = 128
ONE8 = 56.0
STEEP = 2.0 ** 30
FEATURE_SCALE = 2.0 ** 13
REST_SCALE = 2.0 ** 11
LEAK = 0.2
EPS = 1e-5

JG = 4
MASK_RING = 4
ADJ_RING = 4
TPB = 4
IB = TPB * P
ACT_SHARE = (9, 9)


def gat_resnorm(nc, x, adj, weight, att_src, att_dst, bias, out):
    N, K = x.shape
    HEADS, FO = att_src.shape[1], att_src.shape[2]
    HF = HEADS * FO
    NT = N // P
    NB = N // IB
    NG = NT // JG
    V = FO + 1
    SPAN = 4 * V
    HALF = 2 * V
    assert K == P and HF == P and N % IB == 0 and NT % JG == 0 and NG % MASK_RING == 0 and NG % ADJ_RING == 0
    assert NB % 2 == 0 and 3 * SPAN <= 512 and NT // TPB == NB
    XC = NT // ADJ_RING

    dT_dram = nc.dram_tensor("dT_scratch", (HEADS, N), F32).ap()

    with ExitStack() as ctx:
        def sb(name, shape, dt=F32):
            return ctx.enter_context(nc.sbuf_tensor(name, shape, dt))

        def sem(name):
            return ctx.enter_context(nc.semaphore(name))

        ps = ctx.enter_context(nc.psum_tensor("ps", [P, 8, 512], F32))

        feat = sb("feat", [P, NT, HEADS, SPAN], F16)
        adj_f = sb("adj_f", [P, ADJ_RING, JG * IB])
        masks = sb("masks", [P, MASK_RING, JG * HEADS * IB // 4])
        adj8 = sb("adj8", [P, MASK_RING, JG * IB // 4])
        d_rows = sb("d_rows", [P, 2, HEADS * IB])
        s_neg = sb("s_neg", [P, NT, HEADS])
        s_steep = sb("s_steep", [P, NT, HEADS])
        q_all = sb("q_all", [P, NT, HEADS])
        head_size = sb("head_size", [P, HEADS])
        rest = sb("rest", [P, TPB, 12, V])
        sums = sb("sums", [P, TPB, 12, V])
        tail_part = sb("tail_part", [P, TPB, HEADS, V])
        main_part = sb("main_part", [P, TPB, HEADS, V])
        inv_den = sb("inv_den", [P, TPB, HEADS])
        xb = sb("xb", [P, TPB, HF])
        y = sb("y", [P, TPB, HF])
        y_out = sb("y_out", [P, TPB, HF])
        stats = sb("stats", [P, TPB, 6])
        mean_var = sb("mean_var", [P, TPB, 2])
        var_eps = sb("var_eps", [P, TPB])
        rstd = sb("rstd", [P, TPB])
        minus_half = sb("minus_half", [P, TPB])
        bias_rows = sb("bias_rows", [P, HF])
        ident = sb("ident", [P, P])
        ones = sb("ones", [8, P])
        w_nat = sb("w_nat", [P, K])
        att = sb("att", [P, 2])
        head_mask = sb("head_mask", [P, HEADS])
        att_cols = sb("att_cols", [P, 8])
        w_ext = sb("w_ext", [P, HF + 8])
        xT = sb("xT", [P, 2, 512])
        dT_stage = sb("dT_stage", [HEADS, 2, 512])
        sd = sb("sd", [P, NT, 8])
        part_max = sb("part_max", [P, 8])
        row_max = sb("row_max", [8, 1])
        diag_max = sb("diag_max", [8, 8])
        glob = sb("glob", [P, 8])
        inv_size = sb("inv_size", [P, HEADS])
        s_rel = sb("s_rel", [P, NT, HEADS])
        d_rel = sb("d_rel", [P, NT, HEADS])
        wgt = sb("wgt", [P, 2, NT, HEADS])
        wgt_n = sb("wgt_n", [P, 2, NT, HEADS])
        val = d_rows

        xs = adj_f[:, :, :].rearrange("p r (t k) -> p (r t) k", k=K)
        hp = masks[:, :, :].rearrange("p r (t k) -> p (r t) k", k=HF)
        adj_v = adj_f[:, :, :].rearrange("p r (j n) -> p r j n", j=JG)
        m_u8 = masks[:, :, :].bitcast(U8).rearrange("p r (j h n) -> p r j h n", j=JG, h=HEADS)
        m_f8 = masks[:, :, :].bitcast(F8).rearrange("p r (j h n) -> p r j h n", j=JG, h=HEADS)
        m_w = masks[:, :, :].bitcast(I32).rearrange("p r (j h n) -> p r j h n", j=JG, h=HEADS)
        a_u8 = adj8[:, :, :].bitcast(U8)
        a_f8 = adj8[:, :, :].bitcast(F8).rearrange("p r (j n) -> p r j n", j=JG)
        a_w = adj8[:, :, :].bitcast(I32).rearrange("p r (j a n) -> p r j a n", j=JG, a=1)
        d_v = d_rows[:, :, :].rearrange("p b (h n) -> p b h n", h=HEADS)
        by_part = sums[:, :, 0:8, :].rearrange("p t (h q) v -> p t h q v", q=2)

        w_in = sem("w_in")
        x_in = [sem(f"x_in{r}") for r in range(ADJ_RING)]
        consts = sem("consts")
        wt_psum = sem("wt_psum")
        w_ready = sem("w_ready")
        xT_psum = sem("xT_psum")
        xT_sbuf = sem("xT_sbuf")
        proj_psum = sem("proj_psum")
        h_copied = sem("h_copied")
        sd_copied = sem("sd_copied")
        dT_copied = sem("dT_copied")
        dT_out = [sem("dT_out0"), sem("dT_out1")]
        prep = sem("prep")
        max_psum = sem("max_psum")
        exps = sem("exps")
        val_ready = sem("val_ready")
        high_done = sem("high_done")
        val_rest = sem("val_rest")
        rest_done = sem("rest_done")
        den_done = sem("den_done")
        adj_in = [sem(f"adj_in{r}") for r in range(ADJ_RING)]
        adj_used = sem("adj_used")
        d_in = [sem("d_in0"), sem("d_in1")]
        d_used_v = sem("d_used_v")
        d_used_s = sem("d_used_s")
        cmp_s = sem("cmp_s")
        cmp_v = sem("cmp_v")
        masks_ready = sem("masks_ready")
        mask_free = sem("mask_free")
        tile_done = sem("tile_done")
        rest_copied = sem("rest_copied")
        psum_free = sem("psum_free")
        epi = sem("epi")
        xb_in = sem("xb_in")
        xb_ready = sem("xb_ready")
        y_ready = sem("y_ready")
        mv_ready = sem("mv_ready")
        rstd_step = sem("rstd_step")
        norm_done = sem("norm_done")
        stored = sem("stored")

        def chunks(q):
            return slice(q * 16, q * 16 + 16)

        block = ctx.enter_context(nc.Block())

        @block.sync
        def _(sp):
            sp.dma_start(w_nat[:, :], weight).then_inc(w_in, 16)
            with nc.allow_non_contiguous_dma(reason="two columns of 128 values"):
                sp.dma_start(att[:, 0:1], att_src.rearrange("a h (f o) -> (a h f) o", o=1)).then_inc(w_in, 16)
                sp.dma_start(att[:, 1:2], att_dst.rearrange("a h (f o) -> (a h f) o", o=1)).then_inc(w_in, 16)
            sp.dma_start(bias_rows[:, :], bias.rearrange("(a n) -> a n", a=1).to_broadcast([P, HF])).then_inc(w_in, 16)
            for r in range(ADJ_RING):
                sp.dma_start(xs[:, r * XC:(r + 1) * XC, :],
                             x[r * XC * P:(r + 1) * XC * P, :].rearrange("(t p) k -> p t k", p=P)).then_inc(x_in[r], 16)
            for c in range(NT // 4):
                sp.wait_ge(dT_copied, c + 1)
                if c >= 2:
                    sp.wait_ge(dT_out[c % 2], 16 * (c // 2))
                sp.dma_start(dT_dram[:, c * 512:(c + 1) * 512], dT_stage[:, c % 2, :]).then_inc(dT_out[c % 2], 16)

            def load_d(b, parity):
                sp.dma_start(d_v[:, parity, :, :],
                             dT_dram[:, bass.ds(b * IB, IB)].rearrange("(a h) n -> a h n", a=1)
                             .to_broadcast([P, HEADS, IB])).then_inc(d_in[parity], 16)

            def load_xb(b):
                sp.dma_start(xb[:, :, :], x[bass.ds(b * IB, IB), :].rearrange("(t p) k -> p t k", p=P)).then_inc(xb_in, 16)

            def store(b):
                sp.dma_start(out[bass.ds(b * IB, IB), :].rearrange("(t p) k -> p t k", p=P), y_out[:, :, :]).then_inc(stored, 16)

            sp.wait_ge(dT_out[0], 16 * (NT // 8))
            sp.wait_ge(dT_out[1], 16 * (NT // 8))
            sp.wait_ge(rest_done, 8)
            load_d(0, 0)

            def block_loads(b, parity, first=False, last=False):
                for g in range(NG):
                    r = g % ADJ_RING
                    if first and g < ADJ_RING:
                        sp.wait_ge(xT_psum, (g + 1) * XC // 4)
                    else:
                        sp.wait_ge(adj_used, b * NG + (g - ADJ_RING + 1))
                    sp.dma_start(adj_v[:, r, :, :],
                                 adj[g * JG * P:(g + 1) * JG * P, bass.ds(b * IB, IB)]
                                 .rearrange("(j p) n -> p j n", p=P)).then_inc(adj_in[r], 16)
                    if g == NG // 2:
                        if not first:
                            sp.wait_ge(norm_done, b)
                            store(b - 1)
                        load_xb(b)
                        if not last:
                            if not first:
                                sp.wait_ge(d_used_v, b)
                                sp.wait_ge(d_used_s, b)
                            load_d(b + 1, 1 - parity)

            block_loads(0, 0, first=True)
            block_loads(1, 1)
            with sp.Fori(1, NB // 2 - 1) as pair:
                block_loads(pair * 2, 0)
                block_loads(pair * 2 + 1, 1)
            block_loads(NB - 2, 0)
            block_loads(NB - 1, 1, last=True)
            sp.wait_ge(norm_done, NB)
            store(NB - 1)
            sp.wait_ge(stored, 16 * NB)

        @block.gpsimd
        def _(gp):
            gp.memset(ident[:, :], 0.0).then_inc(consts, 1)
            gp.memset(head_mask[:, :], 0.0).then_inc(consts, 1)
            gp.memset(ones[:, :], 1.0).then_inc(consts, 1)
            gp.memset(minus_half[:, :], -0.5).then_inc(consts, 1)
            gp.wait_ge(consts, 4)
            gp.affine_select(out=ident[:, :], in_=ident[:, :], compare_op=ALU.not_equal, fill=1.0,
                             base=0, pattern=[[-1, P]], channel_multiplier=1).then_inc(consts, 1)
            gp.affine_select(out=head_mask[:, :], in_=head_mask[:, :], compare_op=ALU.is_gt, fill=1.0,
                             base=0, pattern=[[FO, HEADS]], channel_multiplier=-1).then_inc(consts, 1)
            gp.wait_ge(consts, 6)
            gp.affine_select(out=head_mask[:, :], in_=head_mask[:, :], compare_op=ALU.is_gt, fill=0.0,
                             base=FO, pattern=[[FO, HEADS]], channel_multiplier=-1).then_inc(consts, 1)

            def per_block(b):
                gp.wait_ge(xb_in, b * 16 + 16)
                gp.tensor_tensor(xb[:, :, :], xb[:, :, :],
                                 bias_rows[:, :].rearrange("p (a n) -> p a n", a=1).to_broadcast([P, TPB, HF]),
                                 ALU.add).then_inc(xb_ready, 1)
                gp.wait_ge(mv_ready, b + 1)
                gp.nop(nofuse=True)
                gp.tensor_scalar(var_eps[:, :], mean_var[:, :, 1], EPS, 1.0, ALU.add, ALU.mult).then_inc(rstd_step, 1)
                gp.wait_ge(rstd_step, b * 2 + 1)
                gp.tensor_tensor(rstd[:, :], var_eps[:, :], minus_half[:, :], ALU.pow).then_inc(rstd_step, 1)

            gp.wait_ge(w_in, 64)
            with gp.Fori(0, NB) as b:
                per_block(b)

        @block.tensor
        def _(pe):
            pe.wait_ge(w_in, 64)
            pe.wait_ge(consts, 5)
            pe.transpose(ps[:, 0, 0:P], w_nat[:, :], ident[:, :]).then_inc(wt_psum, 1)
            pe.wait_ge(w_ready, 1)
            pe.matmul(ps[:, 1, 0:8], w_nat[:, :], att_cols[:, :], start=True, stop=True).then_inc(wt_psum, 1)
            pe.wait_ge(w_ready, 3)

            def turn(c):
                bank = 4 * (c % 2)
                if c % 4 == 0:
                    pe.wait_ge(x_in[c // 4], 16)
                if c >= 2:
                    pe.wait_ge(xT_sbuf, c - 1)
                for t in range(4):
                    mm = pe.transpose(ps[:, bank, t * P:(t + 1) * P], xs[:, 4 * c + t, :], ident[:, :])
                mm.then_inc(xT_psum, 1)

            turn(0)
            for c in range(NT // 4):
                if c + 1 < NT // 4:
                    turn(c + 1)
                bank, half = 4 * (c % 2), c % 2
                pe.wait_ge(xT_sbuf, c + 1)
                if c >= 2:
                    pe.wait_ge(h_copied, c - 1)
                    pe.wait_ge(sd_copied, c - 1)
                    pe.wait_ge(dT_copied, c - 1)
                for t in range(4):
                    tile = xT[:, half, t * P:(t + 1) * P]
                    pe.matmul(ps[:, bank + 1, t * P:(t + 1) * P], tile, w_ext[:, 0:HF], start=True, stop=True)
                    pe.matmul(ps[:, bank + 2, t * 8:(t + 1) * 8], tile, w_ext[:, HF:HF + 8], start=True, stop=True)
                pe.matmul(ps[0:HEADS, bank + 3, :], w_ext[:, HF + 4:HF + 8], xT[:, half, :],
                          start=True, stop=True).then_inc(proj_psum, 1)

            pe.wait_ge(prep, 4)
            pe.transpose(ps[0:8, 0, 0:P], part_max[:, :], ident[:, :]).then_inc(max_psum, 1)
            pe.wait_ge(prep, 6)
            pe.matmul(ps[:, 4, 0:8], ones[:, :], diag_max[:, :], start=True, stop=True).then_inc(max_psum, 1)

            pe.wait_ge(prep, 7)
            pe.wait_ge(h_copied, NT // 4)
            pe.wait_ge(rest_done, 8)
            pe.wait_ge(den_done, 6)
            pe.sem_inc(mask_free, MASK_RING)
            with pe.Fori(0, NB) as b:
                for g in range(NG):
                    slot = g % MASK_RING
                    pe.wait_ge(masks_ready, b * NG + (g + 1))
                    pe.nop(nofuse=True)
                    for t in range(TPB):
                        if g == 0:
                            pe.wait_ge(psum_free, b * TPB + (t + 1))
                            pe.nop(nofuse=True)
                        cols = slice(t * P, (t + 1) * P)
                        for j in range(JG):
                            jt = g * JG + j
                            first, last = jt == 0, jt == NT - 1
                            for h in range(3):
                                pe.matmul(ps[:, 2 * t, h * SPAN:(h + 1) * SPAN], m_f8[:, slot, j, h, cols],
                                          feat[:, jt, h, :], start=first and h == 0, stop=last and h == 2,
                                          skip_group_check=True)
                            pe.matmul(ps[:, 2 * t + 1, 0:SPAN], m_f8[:, slot, j, 3, cols],
                                      feat[:, jt, 3, :], start=first, stop=False, skip_group_check=True)
                            mm = pe.matmul(ps[:, 2 * t + 1, SPAN:SPAN + HEADS * HALF], a_f8[:, slot, j, cols],
                                           feat[:, jt, :, HALF:SPAN], start=False, stop=last, skip_group_check=True)
                        if g == NG - 1:
                            mm.then_inc(tile_done, 1)
                        elif t == TPB - 1:
                            mm.then_inc(mask_free, 1)
                    if g == NG - 1:
                        pe.wait_ge(tile_done, b * TPB + TPB)
                        pe.sem_inc(mask_free, 1)

        @block.scalar
        def _(act):
            for c in range(NT // 4):
                act.wait_ge(proj_psum, c + 1)
                act.activation(hp[:, 4 * c:4 * c + 4, :], ps[:, 4 * (c % 2) + 1, :].rearrange("p (t k) -> p t k", t=4),
                               ACT.Copy).then_inc(h_copied, 1)
            act.wait_ge(prep, 9)
            act.activation(wgt[:, 0, :, :], s_rel[:, :, :], ACT.Exp).then_inc(exps, 1)
            act.activation(wgt[:, 1, :, :], s_rel[:, :, :], ACT.Exp, scale=LEAK).then_inc(exps, 1)
            act.activation(q_all[:, :, :], d_rel[:, :, :], ACT.Exp, scale=1.0 - LEAK).then_inc(exps, 1)
            for n in range(8):
                q, part = n // 2, n % 2
                v = val[:, part, :].rearrange("p (t h f) -> p t h f", t=16, h=HEADS)
                act.wait_ge(val_ready, n + 1)
                act.activation(feat[:, chunks(q), :, part * HALF:part * HALF + FO], v, ACT.Copy).then_inc(high_done, 1)
                act.wait_ge(val_rest, n + 1)
                act.activation(feat[:, chunks(q), :, part * HALF + V:part * HALF + V + FO], v, ACT.Copy,
                               scale=REST_SCALE).then_inc(rest_done, 1)

            def compare(b, parity, g):
                slot = g % MASK_RING
                act.wait_ge(mask_free, b * NG + (g + 1))
                if g == 0:
                    act.wait_ge(d_in[parity], (b - parity) * 8 + 16)
                act.nop(nofuse=True)
                for n in range(ACT_SHARE[g % 2]):
                    j, h = n // HEADS, n % HEADS
                    jt = g * JG + j
                    op = act.activation(m_f8[:, slot, j, h, :], d_v[:, parity, h, :], ACT.Sigmoid,
                                        scale=STEEP, bias=s_steep[:, jt, h:h + 1], saturate=False)
                op.then_inc(cmp_s, 1)
                if g == NG - 1:
                    act.wait_ge(cmp_s, b * NG + NG)
                    act.sem_inc(d_used_s, 1)

            def copy_rest(b):
                for t in range(TPB):
                    act.wait_ge(tile_done, b * TPB + (t + 1))
                    if t == 0:
                        act.wait_ge(psum_free, b * TPB + TPB)
                    for bank in range(2):
                        op = act.activation(rest[:, t, 6 * bank:6 * bank + 6, :],
                                            ps[:, 2 * t + bank, 0:12 * V].rearrange("p (q l v) -> p q l v", l=2, v=V)[:, :, 1, :],
                                            ACT.Copy, scale=1.0 / REST_SCALE)
                    op.then_inc(rest_copied, 1)

            def rotated(b, parity, last=False):
                for g in range(2, NG):
                    compare(b, parity, g)
                if not last:
                    compare(b + 1, 1 - parity, 0)
                copy_rest(b)
                if not last:
                    compare(b + 1, 1 - parity, 1)

            act.preload_act_table(ACT.Sigmoid)
            compare(0, 0, 0)
            compare(0, 0, 1)
            with act.Fori(0, NB // 2 - 1) as pair:
                rotated(pair * 2, 0)
                rotated(pair * 2 + 1, 1)
            rotated(NB - 2, 0)
            rotated(NB - 1, 1, last=True)

        @block.vector
        def _(dve):
            dve.wait_ge(w_in, 64)
            dve.wait_ge(consts, 7)
            dve.tensor_scalar(att_cols[:, 0:HEADS], head_mask[:, :], att[:, 0:1], None, ALU.mult)
            dve.tensor_scalar(att_cols[:, HEADS:8], head_mask[:, :], att[:, 1:2], None, ALU.mult).then_inc(w_ready, 1)
            dve.wait_ge(wt_psum, 1)
            dve.tensor_copy(w_ext[:, 0:HF], ps[:, 0, 0:P]).then_inc(w_ready, 1)
            dve.wait_ge(wt_psum, 2)
            dve.tensor_copy(w_ext[:, HF:HF + 8], ps[:, 1, 0:8]).then_inc(w_ready, 1)
            for c in range(NT // 4 + 1):
                bank, half = 4 * (c % 2), c % 2
                if c < NT // 4:
                    dve.wait_ge(xT_psum, c + 1)
                    if c >= 2:
                        dve.wait_ge(proj_psum, c - 1)
                    dve.tensor_copy(xT[:, half, :], ps[:, bank, :]).then_inc(xT_sbuf, 1)
                if c >= 1:
                    e = c - 1
                    bank, half = 4 * (e % 2), e % 2
                    dve.wait_ge(proj_psum, e + 1)
                    dve.tensor_copy(sd[:, 4 * e:4 * e + 4, :],
                                    ps[:, bank + 2, 0:32].rearrange("p (t k) -> p t k", t=4)).then_inc(sd_copied, 1)
                    if e >= 2:
                        dve.wait_ge(dT_out[half], 16 * (e // 2))
                    dve.tensor_copy(dT_stage[:, half, :], ps[0:HEADS, bank + 3, :]).then_inc(dT_copied, 1)
            dve.wait_ge(sd_copied, NT // 4)
            dve.wait_ge(h_copied, NT // 4)
            for h in range(HEADS):
                dve.tensor_reduce(part_max[:, h:h + 1], hp[:, :, h * FO:(h + 1) * FO], AX.XY, ALU.max,
                                  apply_absolute_value=True).then_inc(prep, 1) if h < 3 else \
                    dve.tensor_reduce(part_max[:, h:h + 1], hp[:, :, h * FO:(h + 1) * FO], AX.XY, ALU.max,
                                      apply_absolute_value=True)
            dve.tensor_reduce(part_max[:, HEADS:8], sd[:, :, 0:HEADS].rearrange("p t h -> p h t"), AX.X,
                              ALU.max).then_inc(prep, 1)
            dve.wait_ge(max_psum, 1)
            dve.tensor_reduce(row_max[:, :], ps[0:8, 0, 0:P], AX.X, ALU.max).then_inc(prep, 1)
            dve.wait_ge(prep, 5)
            dve.tensor_scalar(diag_max[:, :], ident[0:8, 0:8], row_max[:, 0:1], None, ALU.mult).then_inc(prep, 1)
            dve.wait_ge(max_psum, 2)
            dve.tensor_copy(glob[:, :], ps[:, 4, 0:8]).then_inc(prep, 1)
            dve.wait_ge(prep, 7)
            dve.tensor_tensor(s_rel[:, :, :], sd[:, :, 0:HEADS],
                              glob[:, HEADS:8].rearrange("p (a h) -> p a h", a=1).to_broadcast([P, NT, HEADS]),
                              ALU.subtract).then_inc(prep, 1)
            dve.tensor_tensor(d_rel[:, :, :], sd[:, :, HEADS:8],
                              glob[:, HEADS:8].rearrange("p (a h) -> p a h", a=1).to_broadcast([P, NT, HEADS]),
                              ALU.add).then_inc(prep, 1)
            dve.tensor_scalar(head_size[:, :], glob[:, 0:HEADS], 1e-30, None, ALU.max).then_inc(prep, 1)
            dve.tensor_scalar(s_neg[:, :, :], sd[:, :, 0:HEADS], -1.0, None, ALU.mult).then_inc(prep, 1)
            dve.tensor_scalar(s_steep[:, :, :], sd[:, :, 0:HEADS], STEEP, None, ALU.mult).then_inc(prep, 1)
            dve.wait_ge(prep, 10)
            dve.reciprocal(inv_size[:, :], head_size[:, :]).then_inc(prep, 1)
            dve.wait_ge(exps, 2)
            dve.tensor_scalar(wgt[:, :, :, :], wgt[:, :, :, :], FEATURE_SCALE, None, ALU.mult).then_inc(prep, 1)
            dve.wait_ge(prep, 14)
            dve.tensor_tensor(wgt_n[:, :, :, :].rearrange("p q t h -> p (q t) h"),
                              wgt[:, :, :, :].rearrange("p q t h -> p (q t) h"),
                              inv_size[:, :].rearrange("p (a h) -> p a h", a=1).to_broadcast([P, 2 * NT, HEADS]),
                              ALU.mult).then_inc(prep, 1)
            dve.wait_ge(prep, 15)
            for part in range(2):
                dve.tensor_copy(feat[:, :, :, part * HALF + FO], wgt[:, part, :, :]).then_inc(den_done, 1)
                dve.wait_ge(den_done, 3 * part + 1)
                dve.tensor_tensor(wgt[:, part, :, :], wgt[:, part, :, :], feat[:, :, :, part * HALF + FO],
                                  ALU.subtract).then_inc(den_done, 1)
                dve.wait_ge(den_done, 3 * part + 2)
                dve.tensor_scalar(feat[:, :, :, part * HALF + V + FO], wgt[:, part, :, :], REST_SCALE, None,
                                  ALU.mult).then_inc(den_done, 1)
            for n in range(10):
                if n < 8:
                    q, part = n // 2, n % 2
                    v = val[:, part, :].rearrange("p (t f) -> p t f", f=FO)
                    if n >= 2:
                        dve.wait_ge(rest_done, n - 1)
                    dve.tensor_tensor(v, hp[:, chunks(q), :].rearrange("p t (h f) -> p (t h) f", h=HEADS),
                                      wgt_n[:, part, chunks(q), :].rearrange("p t (h o) -> p (t h) o", o=1)
                                      .to_broadcast([P, 16 * HEADS, FO]), ALU.mult).then_inc(val_ready, 1)
                if n >= 1 and n - 1 < 8:
                    q, part = (n - 1) // 2, (n - 1) % 2
                    v = val[:, part, :].rearrange("p (t h f) -> p t h f", t=16, h=HEADS)
                    dve.wait_ge(high_done, n)
                    dve.wait_ge(val_ready, n)
                    dve.tensor_tensor(v, v, feat[:, chunks(q), :, part * HALF:part * HALF + FO],
                                      ALU.subtract).then_inc(val_rest, 1)

            dve.sem_inc(psum_free, TPB)

            def masks_of(b, parity, g):
                slot, r = g % MASK_RING, g % ADJ_RING
                dve.wait_ge(mask_free, b * NG + (g + 1))
                dve.wait_ge(adj_in[r], b * (16 * NG // ADJ_RING) + 16 * (g // ADJ_RING + 1))
                dve.tensor_scalar(a_u8[:, slot, :], adj_f[:, r, :], ONE8, None, ALU.mult).then_inc(adj_used, 1)
                if g == 0:
                    dve.wait_ge(d_in[parity], (b - parity) * 8 + 16)
                for n in range(ACT_SHARE[g % 2], JG * HEADS):
                    j, h = n // HEADS, n % HEADS
                    jt = g * JG + j
                    op = dve.tensor_scalar(m_u8[:, slot, j, h, :], d_v[:, parity, h, :], s_neg[:, jt, h:h + 1], ONE8,
                                           ALU.is_gt, ALU.mult)
                op.then_inc(cmp_v, 1)
                if g == NG - 1:
                    dve.wait_ge(cmp_v, b * NG + NG)
                    dve.sem_inc(d_used_v, 1)
                dve.wait_ge(cmp_v, b * NG + (g + 1))
                dve.wait_ge(cmp_s, b * NG + (g + 1))
                dve.wait_ge(adj_used, b * NG + (g + 1))
                dve.tensor_tensor(m_w[:, slot], m_w[:, slot], a_w[:, slot].to_broadcast([P, JG, HEADS, IB // 4]),
                                  ALU.bitwise_and).then_inc(masks_ready, 1)

            EPI = 5

            def finish_sums(b):
                for t in range(TPB):
                    dve.wait_ge(rest_copied, b * TPB + (t + 1))
                    for bank in range(2):
                        op = dve.tensor_tensor(sums[:, t, 6 * bank:6 * bank + 6, :],
                                               ps[:, 2 * t + bank, 0:12 * V].rearrange("p (q l v) -> p q l v", l=2, v=V)[:, :, 0, :],
                                               rest[:, t, 6 * bank:6 * bank + 6, :], ALU.add)
                    op.then_inc(psum_free, 1)
                dve.wait_ge(psum_free, b * TPB + 2 * TPB)
                dve.tensor_tensor(tail_part[:, :, :, :], sums[:, :, 8:12, :], by_part[:, :, :, 1, :], ALU.subtract).then_inc(epi, 1)
                dve.tensor_tensor(main_part[:, :, :, :], by_part[:, :, :, 0, :],
                                  q_all[:, bass.ds(b * TPB, TPB), :].rearrange("p t (h o) -> p t h o", o=1)
                                  .to_broadcast([P, TPB, HEADS, V]), ALU.mult).then_inc(epi, 1)
                dve.wait_ge(epi, b * EPI + 2)
                dve.tensor_tensor(main_part[:, :, :, :], main_part[:, :, :, :], tail_part[:, :, :, :], ALU.add).then_inc(epi, 1)
                dve.wait_ge(epi, b * EPI + 3)
                dve.reciprocal(inv_den[:, :, :], main_part[:, :, :, FO]).then_inc(epi, 1)
                dve.wait_ge(epi, b * EPI + 4)
                dve.tensor_tensor(inv_den[:, :, :], inv_den[:, :, :],
                                  head_size[:, :].rearrange("p (a h) -> p a h", a=1).to_broadcast([P, TPB, HEADS]),
                                  ALU.mult).then_inc(epi, 1)
                dve.wait_ge(epi, b * EPI + 5)
                dve.tensor_tensor(y[:, :, :].rearrange("p t (h f) -> p t h f", h=HEADS), main_part[:, :, :, 0:FO],
                                  inv_den[:, :, :].rearrange("p t (h o) -> p t h o", o=1)
                                  .to_broadcast([P, TPB, HEADS, FO]), ALU.mult).then_inc(y_ready, 1)
                dve.wait_ge(y_ready, b * 3 + 1)
                dve.wait_ge(xb_ready, b + 1)
                dve.tensor_tensor(y[:, :, :], y[:, :, :], xb[:, :, :], ALU.add).then_inc(y_ready, 1)
                dve.wait_ge(y_ready, b * 3 + 2)
                for t in range(TPB):
                    op = dve.bn_stats(stats[:, t, :], y[:, t, :])
                op.then_inc(y_ready, 1)
                dve.wait_ge(y_ready, b * 3 + 3)
                dve.nop(nofuse=True)
                for t in range(TPB):
                    op = dve.bn_aggr(mean_var[:, t, :], stats[:, t, :])
                op.then_inc(mv_ready, 1)

            def normalise(b, first=False):
                dve.wait_ge(rstd_step, b * 2 + 2)
                if not first:
                    dve.wait_ge(stored, b * 16)
                for t in range(TPB):
                    op = dve.tensor_scalar(y_out[:, t, :], y[:, t, :], mean_var[:, t, 0:1], rstd[:, t:t + 1],
                                           ALU.subtract, ALU.mult)
                op.then_inc(norm_done, 1)

            def rotated(b, parity, first=False, last=False):
                for g in range(2, NG):
                    masks_of(b, parity, g)
                if not last:
                    masks_of(b + 1, 1 - parity, 0)
                finish_sums(b)
                if not last:
                    masks_of(b + 1, 1 - parity, 1)
                normalise(b, first)

            masks_of(0, 0, 0)
            masks_of(0, 0, 1)
            rotated(0, 0, first=True)
            rotated(1, 1)
            with dve.Fori(1, NB // 2 - 1) as pair:
                rotated(pair * 2, 0)
                rotated(pair * 2 + 1, 1)
            rotated(NB - 2, 0)
            rotated(NB - 1, 1, last=True)


_INS = ["x", "adj", "L0_gnn_weight", "L0_gnn_att_src", "L0_gnn_att_dst", "L0_gnn_bias"]


def kernel(**inputs):
    import numpy as np
    import concourse.bacc as bacc
    from concourse.bass_utils import run_bass_kernel_spmd

    nc = bacc.Bacc("TRN2", target_bir_lowering=False, num_devices=1)
    arrays, args = {}, []
    for name in _INS:
        a = np.ascontiguousarray(inputs[name])
        arrays[f"in_{name}"] = a
        args.append(nc.dram_tensor(f"in_{name}", a.shape, mybir.dt.from_np(a.dtype), kind="ExternalInput").ap())
    out = nc.dram_tensor("out_x", arrays["in_x"].shape, F32, kind="ExternalOutput").ap()
    gat_resnorm(nc, *args, out)
    r = run_bass_kernel_spmd(nc, [arrays], core_ids=[0])
    return r.results[0]["out_x"]
```

```python
from contextlib import ExitStack

import concourse.bass as bass
from concourse import mybir

ALU = mybir.AluOpType
ACT = mybir.ActivationFunctionType
AX = mybir.AxisListType
F32 = mybir.dt.float32
F16 = mybir.dt.float16
F8 = mybir.dt.float8e4
U8 = mybir.dt.uint8
I32 = mybir.dt.int32

P = 128
ONE8 = 56.0
ADJ8 = 1.875
STEEP = 2.0 ** 30
FEATURE_SCALE = 2.0 ** 13
REST_SCALE = 2.0 ** 11
LEAK = 0.2
EPS = 1e-5

JG = 4
RING = 4
TPB = 4
IB = TPB * P
ACT_SHARE = (9, 9, 9, 8)
AHEAD = 6
EVAC_GROUP = 2


def gat_resnorm(nc, x, adj, weight, att_src, att_dst, bias, out):
    N, K = x.shape
    HEADS, FO = att_src.shape[1], att_src.shape[2]
    HF = HEADS * FO
    NT = N // P
    NB = N // IB
    NG = NT // JG
    V = FO + 1
    SPAN = 4 * V
    HALF = 2 * V
    assert K == P and HF == P and N % IB == 0 and NT % JG == 0 and NG % RING == 0
    assert NB % 2 == 0 and 3 * SPAN <= 512 and NT // TPB == NB
    CH = NT // RING
    STEPS = NT // 4

    dT_dram = nc.dram_tensor("dT_scratch", (HEADS, N), F32).ap()

    with ExitStack() as ctx:
        def sb(name, shape, dt=F32):
            return ctx.enter_context(nc.sbuf_tensor(name, shape, dt))

        def sem(name):
            return ctx.enter_context(nc.semaphore(name))

        ps = ctx.enter_context(nc.psum_tensor("ps", [P, 8, 512], F32))

        feat = sb("feat", [P, NT, HEADS, SPAN], F16)
        adj_f = sb("adj_f", [P, RING, JG * IB])
        masks = sb("masks", [P, RING, JG * IB])
        d_rows = sb("d_rows", [P, 2, HEADS * IB])
        s_neg = sb("s_neg", [P, NT, HEADS])
        s_steep = sb("s_steep", [P, NT, HEADS])
        q_all = sb("q_all", [P, NT, HEADS])
        head_size = sb("head_size", [P, HEADS])
        work = sb("work", [P, 2, TPB * 12 * V])
        tail_part = sb("tail_part", [P, TPB, HEADS, V])
        main_part = sb("main_part", [P, TPB, HEADS, V])
        inv_den = sb("inv_den", [P, TPB, HEADS])
        xb = sb("xb", [P, TPB, HF])
        y = sb("y", [P, TPB, HF])
        y_out = sb("y_out", [P, TPB, HF])
        stats = sb("stats", [P, TPB, 6])
        mean_var = sb("mean_var", [P, TPB, 2])
        var_eps = sb("var_eps", [P, TPB])
        rstd = sb("rstd", [P, TPB])
        minus_half = sb("minus_half", [P, TPB])
        bias_rows = sb("bias_rows", [P, HF])
        ident = sb("ident", [P, P])
        ones = sb("ones", [8, P])
        w_nat = sb("w_nat", [P, K])
        att = sb("att", [P, 2])
        head_mask = sb("head_mask", [P, HEADS])
        att_cols = sb("att_cols", [P, 8])
        w_ext = sb("w_ext", [P, HF + 8])
        xT = sb("xT", [P, 2, 512])
        d_cols = sb("d_cols", [P, HEADS, NT])
        dT = sb("dT", [P, 2, P])
        tile_max = sb("tile_max", [P, NT, HEADS])
        sd = sb("sd", [P, NT, 8])
        part_max = sb("part_max", [P, 8])
        row_max = sb("row_max", [8, 1])
        diag_max = sb("diag_max", [8, 8])
        glob = sb("glob", [P, 8])
        inv_size = sb("inv_size", [P, HEADS])
        s_rel = sb("s_rel", [P, NT, HEADS])
        d_rel = sb("d_rel", [P, NT, HEADS])
        wgt = sb("wgt", [P, 2, NT, HEADS])
        wgt_n = sb("wgt_n", [P, 2, NT, HEADS])
        val = sb("val", [P, 2, CH * HF])

        vals = [val[:, 0, :], val[:, 1, :], d_rows[:, 1, :]]
        val_gp = work[:, :, :].rearrange("p w n -> p (w n)")[:, 0:CH * HF]
        rest = work[:, 0, :].rearrange("p (t q v) -> p t q v", t=TPB, v=V)
        sums = work[:, 1, :].rearrange("p (t q v) -> p t q v", t=TPB, v=V)
        xs = adj_f[:, :, :].rearrange("p r (t k) -> p (r t) k", k=K)
        hp = masks[:, :, :].rearrange("p r (t k) -> p (r t) k", k=HF)
        adj_v = adj_f[:, :, :].rearrange("p r (j n) -> p r j n", j=JG)
        m_u8 = masks[:, :, :].bitcast(U8).rearrange("p r (j n h) -> p r j n h", j=JG, h=HEADS)
        m_f8 = masks[:, :, :].bitcast(F8).rearrange("p r (j n h) -> p r j n h", j=JG, h=HEADS)
        a_f8 = adj_f[:, :, :].bitcast(F8).rearrange("p r (j n h) -> p r j n h", j=JG, h=4)
        d_v = d_rows[:, :, :].rearrange("p b (h n) -> p b h n", h=HEADS)
        by_part = sums[:, :, 0:8, :].rearrange("p t (h q) v -> p t h q v", q=2)

        w_in = sem("w_in")
        x_in = [sem(f"x_in{r}") for r in range(RING)]
        consts = sem("consts")
        wt_psum = sem("wt_psum")
        w_ready = sem("w_ready")
        xT_psum = sem("xT_psum")
        xT_sbuf = sem("xT_sbuf")
        proj_psum = sem("proj_psum")
        h_copied = sem("h_copied")
        sd_copied = sem("sd_copied")
        d_turn = sem("d_turn")
        dT_out = sem("dT_out")
        tile_maxed = sem("tile_maxed")
        prep = sem("prep")
        max_psum = sem("max_psum")
        exps = sem("exps")
        wgt_ready = sem("wgt_ready")
        val_ready = {"v": sem("val_ready_v"), "g": sem("val_ready_g")}
        val_rest = {"v": sem("val_rest_v"), "g": sem("val_rest_g")}
        feat_step = sem("feat_step")
        den_done = sem("den_done")
        adj_in = [sem(f"adj_in{r}") for r in range(RING)]
        d_in = [sem("d_in0"), sem("d_in1")]
        d_used_v = sem("d_used_v")
        d_used_s = sem("d_used_s")
        cmp_s = sem("cmp_s")
        cmp_v = sem("cmp_v")
        masks_ready = sem("masks_ready")
        slot_free = sem("slot_free")
        tile_done = sem("tile_done")
        rest_copied = sem("rest_copied")
        psum_free = sem("psum_free")
        epi = sem("epi")
        xb_in = sem("xb_in")
        xb_ready = sem("xb_ready")
        y_ready = sem("y_ready")
        mv_ready = sem("mv_ready")
        rstd_step = sem("rstd_step")
        norm_done = sem("norm_done")
        stored = sem("stored")

        PIECES = 2 * RING
        GP_FROM = PIECES - 2
        FEAT_ORDER = ["H0", "H1", "R0", "H6", "H2", "R1", "H3", "R2", "R6", "H4", "R3", "H7", "H5", "R4", "R5", "R7"]

        def feat_at(step):
            return FEAT_ORDER.index(step) + 1

        def piece(n):
            return slice(n // 2 * CH, n // 2 * CH + CH), n % 2, vals[n % 3] if n < GP_FROM else val_gp

        def multiply(eng, n):
            tiles, part, v = piece(n)
            return eng.tensor_tensor(v.rearrange("p (t f) -> p t f", f=FO),
                                     hp[:, tiles, :].rearrange("p t (h f) -> p (t h) f", h=HEADS),
                                     wgt_n[:, part, tiles, :].rearrange("p t (h o) -> p (t h) o", o=1)
                                     .to_broadcast([P, CH * HEADS, FO]), ALU.mult)

        def subtract_high(eng, n):
            tiles, part, v = piece(n)
            v = v.rearrange("p (t h f) -> p t h f", t=CH, h=HEADS)
            return eng.tensor_tensor(v, v, feat[:, tiles, :, part * HALF:part * HALF + FO], ALU.subtract)

        block = ctx.enter_context(nc.Block())

        @block.sync
        def _(sp):
            sp.dma_start(w_nat[:, :], weight).then_inc(w_in, 16)
            with nc.allow_non_contiguous_dma(reason="two columns of 128 values"):
                sp.dma_start(att[:, 0:1], att_src.rearrange("a h (f o) -> (a h f) o", o=1)).then_inc(w_in, 16)
                sp.dma_start(att[:, 1:2], att_dst.rearrange("a h (f o) -> (a h f) o", o=1)).then_inc(w_in, 16)
            sp.dma_start(bias_rows[:, :], bias.rearrange("(a n) -> a n", a=1).to_broadcast([P, HF])).then_inc(w_in, 16)
            for r in range(RING):
                sp.dma_start(xs[:, r * CH:(r + 1) * CH, :],
                             x[r * CH * P:(r + 1) * CH * P, :].rearrange("(t p) k -> p t k", p=P)).then_inc(x_in[r], 16)
            sp.wait_ge(d_turn, 4)
            for k in range(2):
                sp.dma_start(dT_dram.rearrange("h (t p) -> (h t) p", p=P)[k * P:(k + 1) * P, :],
                             dT[:, k, :]).then_inc(dT_out, 16)

            def load_d(b, parity):
                sp.dma_start(d_v[:, parity, :, :],
                             dT_dram[:, bass.ds(b * IB, IB)].rearrange("(a h) n -> a h n", a=1)
                             .to_broadcast([P, HEADS, IB])).then_inc(d_in[parity], 16)

            def load_xb(b):
                sp.dma_start(xb[:, :, :], x[bass.ds(b * IB, IB), :].rearrange("(t p) k -> p t k", p=P)).then_inc(xb_in, 16)

            def store(b):
                sp.dma_start(out[bass.ds(b * IB, IB), :].rearrange("(t p) k -> p t k", p=P), y_out[:, :, :]).then_inc(stored, 16)

            sp.wait_ge(dT_out, 32)
            load_d(0, 0)

            def block_loads(b, parity, first=False, last=False):
                for g in range(NG):
                    r = g % RING
                    if first and g < RING:
                        sp.wait_ge(xT_psum, (g + 1) * CH // 4)
                    else:
                        sp.wait_ge(slot_free, b * NG + (g + 1))
                    sp.dma_start(adj_v[:, r, :, :],
                                 adj[g * JG * P:(g + 1) * JG * P, bass.ds(b * IB, IB)]
                                 .rearrange("(j p) n -> p j n", p=P)).then_inc(adj_in[r], 16)
                    if g == NG // 2:
                        if not first:
                            sp.wait_ge(norm_done, b)
                            store(b - 1)
                        load_xb(b)
                        if not last:
                            if first:
                                sp.wait_ge(feat_step, len(FEAT_ORDER))
                            else:
                                sp.wait_ge(d_used_v, b)
                                sp.wait_ge(d_used_s, b)
                            load_d(b + 1, 1 - parity)

            block_loads(0, 0, first=True)
            block_loads(1, 1)
            with sp.Fori(1, NB // 2 - 1) as pair:
                block_loads(pair * 2, 0)
                block_loads(pair * 2 + 1, 1)
            block_loads(NB - 2, 0)
            block_loads(NB - 1, 1, last=True)
            sp.wait_ge(norm_done, NB)
            store(NB - 1)
            sp.wait_ge(stored, 16 * NB)

        @block.gpsimd
        def _(gp):
            gp.memset(ident[:, :], 0.0).then_inc(consts, 1)
            gp.memset(head_mask[:, :], 0.0).then_inc(consts, 1)
            gp.memset(ones[:, :], 1.0).then_inc(consts, 1)
            gp.memset(minus_half[:, :], -0.5).then_inc(consts, 1)
            gp.wait_ge(consts, 4)
            gp.affine_select(out=ident[:, :], in_=ident[:, :], compare_op=ALU.not_equal, fill=1.0,
                             base=0, pattern=[[-1, P]], channel_multiplier=1).then_inc(consts, 1)
            gp.affine_select(out=head_mask[:, :], in_=head_mask[:, :], compare_op=ALU.is_gt, fill=1.0,
                             base=0, pattern=[[FO, HEADS]], channel_multiplier=-1).then_inc(consts, 1)
            gp.wait_ge(consts, 6)
            gp.affine_select(out=head_mask[:, :], in_=head_mask[:, :], compare_op=ALU.is_gt, fill=0.0,
                             base=FO, pattern=[[FO, HEADS]], channel_multiplier=-1).then_inc(consts, 1)

            def per_block(b):
                gp.wait_ge(xb_in, b * 16 + 16)
                gp.tensor_tensor(xb[:, :, :], xb[:, :, :],
                                 bias_rows[:, :].rearrange("p (a n) -> p a n", a=1).to_broadcast([P, TPB, HF]),
                                 ALU.add).then_inc(xb_ready, 1)
                gp.wait_ge(mv_ready, b + 1)
                gp.nop(nofuse=True)
                gp.tensor_scalar(var_eps[:, :], mean_var[:, :, 1], EPS, 1.0, ALU.add, ALU.mult).then_inc(rstd_step, 1)
                gp.wait_ge(rstd_step, b * 2 + 1)
                gp.tensor_tensor(rstd[:, :], var_eps[:, :], minus_half[:, :], ALU.pow).then_inc(rstd_step, 1)

            gp.wait_ge(wgt_ready, 1)
            for n in range(GP_FROM, PIECES):
                if n > GP_FROM:
                    gp.wait_ge(feat_step, feat_at(f"R{n - 1}"))
                multiply(gp, n).then_inc(val_ready["g"], 1)
                gp.wait_ge(val_ready["g"], n - GP_FROM + 1)
                gp.wait_ge(feat_step, feat_at(f"H{n}"))
                subtract_high(gp, n).then_inc(val_rest["g"], 1)

            gp.wait_ge(w_in, 64)
            with gp.Fori(0, NB) as b:
                per_block(b)

        @block.tensor
        def _(pe):
            pe.wait_ge(w_in, 64)
            pe.wait_ge(consts, 5)
            pe.transpose(ps[:, 0, 0:P], w_nat[:, :], ident[:, :]).then_inc(wt_psum, 1)
            pe.wait_ge(w_ready, 1)
            pe.matmul(ps[:, 1, 0:8], w_nat[:, :], att_cols[:, :], start=True, stop=True).then_inc(wt_psum, 1)
            pe.wait_ge(w_ready, 3)

            def turn(c):
                bank = 4 * (c % 2)
                if c % 4 == 0:
                    pe.wait_ge(x_in[c // 4], 16)
                if c >= 2:
                    pe.wait_ge(xT_sbuf, c - 1)
                for t in range(4):
                    mm = pe.transpose(ps[:, bank, t * P:(t + 1) * P], xs[:, 4 * c + t, :], ident[:, :])
                mm.then_inc(xT_psum, 1)

            turn(0)
            for c in range(STEPS):
                if c + 1 < STEPS:
                    turn(c + 1)
                bank, half = 4 * (c % 2), c % 2
                pe.wait_ge(xT_sbuf, c + 1)
                if c >= 2:
                    pe.wait_ge(h_copied, c - 1)
                    pe.wait_ge(sd_copied, c - 1)
                for t in range(4):
                    mm = pe.matmul(ps[:, bank + 1 + t // 3, t % 3 * (HF + 8):(t % 3 + 1) * (HF + 8)],
                                   xT[:, half, t * P:(t + 1) * P], w_ext[:, :], start=True, stop=True)
                mm.then_inc(proj_psum, 1)

            pe.wait_ge(d_turn, 1)
            for k in range(2):
                mm = pe.transpose(ps[:, 3, k * P:(k + 1) * P],
                                  d_cols[:, :, :].rearrange("p h t -> p (h t)")[:, k * P:(k + 1) * P], ident[:, :])
            mm.then_inc(d_turn, 1)

            pe.wait_ge(prep, 2)
            pe.transpose(ps[0:8, 0, 0:P], part_max[:, :], ident[:, :]).then_inc(max_psum, 1)
            pe.wait_ge(prep, 4)
            pe.matmul(ps[:, 4, 0:8], ones[:, :], diag_max[:, :], start=True, stop=True).then_inc(max_psum, 1)

            pe.wait_ge(prep, 5)
            pe.wait_ge(d_turn, 4)
            pe.wait_ge(feat_step, len(FEAT_ORDER))
            pe.wait_ge(den_done, 6)
            pe.sem_inc(slot_free, RING)
            with pe.Fori(0, NB) as b:
                for g in range(NG):
                    slot = g % RING
                    pe.wait_ge(masks_ready, b * NG + (g + 1))
                    pe.nop(nofuse=True)
                    for t in range(TPB):
                        if g == 0:
                            pe.wait_ge(psum_free, b * TPB + (t + 1))
                            pe.nop(nofuse=True)
                        cols = slice(t * P, (t + 1) * P)
                        for j in range(JG):
                            jt = g * JG + j
                            first, last = jt == 0, jt == NT - 1
                            for h in range(3):
                                pe.matmul(ps[:, 2 * t, h * SPAN:(h + 1) * SPAN], m_f8[:, slot, j, cols, h],
                                          feat[:, jt, h, :], start=first and h == 0, stop=last and h == 2,
                                          skip_group_check=True)
                            pe.matmul(ps[:, 2 * t + 1, 0:SPAN], m_f8[:, slot, j, cols, 3],
                                      feat[:, jt, 3, :], start=first, stop=False, skip_group_check=True)
                            mm = pe.matmul(ps[:, 2 * t + 1, SPAN:SPAN + HEADS * HALF], a_f8[:, slot, j, cols, 3],
                                           feat[:, jt, :, HALF:SPAN], start=False, stop=last, skip_group_check=True)
                        if g == NG - 1:
                            mm.then_inc(tile_done, 1)
                        elif t == TPB - 1:
                            mm.then_inc(slot_free, 1)
                    if g == NG - 1:
                        pe.wait_ge(tile_done, b * TPB + TPB)
                        pe.sem_inc(slot_free, 1)

        @block.scalar
        def _(act):
            for c in range(STEPS):
                bank = 4 * (c % 2)
                act.wait_ge(proj_psum, c + 1)
                for t, n in ((0, 3), (3, 1)):
                    from_psum = ps[:, bank + 1 + t // 3, 0:n * (HF + 8)].rearrange("p (t k) -> p t k", t=n)
                    tiles = slice(4 * c + t, 4 * c + t + n)
                    op_h = act.activation(hp[:, tiles, :], from_psum[:, :, 0:HF], ACT.Copy)
                    if t:
                        op_h.then_inc(h_copied, 1)
                    op_sd = act.activation(sd[:, tiles, :], from_psum[:, :, HF:HF + 8], ACT.Copy)
                    if t:
                        op_sd.then_inc(sd_copied, 1)
            act.wait_ge(prep, 6)
            act.activation(wgt[:, 0, :, :], s_rel[:, :, :], ACT.Exp).then_inc(exps, 1)
            act.activation(wgt[:, 1, :, :], s_rel[:, :, :], ACT.Exp, scale=LEAK).then_inc(exps, 1)
            act.wait_ge(prep, 7)
            act.activation(q_all[:, :, :], d_rel[:, :, :], ACT.Exp, scale=1.0 - LEAK).then_inc(exps, 1)
            for step in FEAT_ORDER:
                n = int(step[1])
                tiles, part, v = piece(n)
                maker, count = ("v", n + 1) if n < GP_FROM else ("g", n - GP_FROM + 1)
                v = v.rearrange("p (t h f) -> p t h f", t=CH, h=HEADS)
                if step[0] == "H":
                    act.wait_ge(val_ready[maker], count)
                    act.activation(feat[:, tiles, :, part * HALF:part * HALF + FO], v, ACT.Copy).then_inc(feat_step, 1)
                else:
                    act.wait_ge(val_rest[maker], count)
                    act.activation(feat[:, tiles, :, part * HALF + V:part * HALF + V + FO], v, ACT.Copy,
                                   scale=REST_SCALE).then_inc(feat_step, 1)

            def compare(b, parity, g, of=None):
                slot = g % RING
                act.wait_ge(slot_free, b * NG + (g + 1))
                if g == 0:
                    act.wait_ge(d_in[parity], (b - parity) * 8 + 16)
                act.nop(nofuse=True)
                share = ACT_SHARE[g % len(ACT_SHARE)]
                for n in range(share):
                    if of is not None and n % (share // TPB) == 0 and n // (share // TPB) < TPB:
                        copy_rest(of, n // (share // TPB))
                    j, h = n // HEADS, n % HEADS
                    jt = g * JG + j
                    op = act.activation(m_f8[:, slot, j, :, h], d_v[:, parity, h, :], ACT.Sigmoid,
                                        scale=STEEP, bias=s_steep[:, jt, h:h + 1], saturate=False)
                op.then_inc(cmp_s, 1)
                if g == NG - 1:
                    act.wait_ge(cmp_s, b * NG + NG)
                    act.sem_inc(d_used_s, 1)

            def copy_rest(b, t):
                act.wait_ge(tile_done, b * TPB + (t + 1))
                if t == 0:
                    act.wait_ge(psum_free, b * TPB + TPB)
                for bank in range(2):
                    op = act.activation(rest[:, t, 6 * bank:6 * bank + 6, :],
                                        ps[:, 2 * t + bank, 0:12 * V].rearrange("p (q l v) -> p q l v", l=2, v=V)[:, :, 1, :],
                                        ACT.Copy, scale=1.0 / REST_SCALE)
                op.then_inc(rest_copied, 1)

            def rotated(b, parity, last=False):
                for g in range(AHEAD, NG):
                    compare(b, parity, g)
                if last:
                    for t in range(TPB):
                        copy_rest(b, t)
                else:
                    for g in range(AHEAD):
                        compare(b + 1, 1 - parity, g, of=b if g == EVAC_GROUP else None)

            act.preload_act_table(ACT.Sigmoid)
            for g in range(AHEAD):
                compare(0, 0, g)
            with act.Fori(0, NB // 2 - 1) as pair:
                rotated(pair * 2, 0)
                rotated(pair * 2 + 1, 1)
            rotated(NB - 2, 0)
            rotated(NB - 1, 1, last=True)

        def largest(dve, q):
            dve.wait_ge(h_copied, 4 * q + 4)
            dve.tensor_reduce(tile_max[:, q * CH:(q + 1) * CH, :].rearrange("p t h -> p (t h)"),
                              hp[:, q * CH:(q + 1) * CH, :].rearrange("p t (h f) -> p (t h) f", h=HEADS), AX.X, ALU.max,
                              apply_absolute_value=True).then_inc(tile_maxed, 1)

        @block.vector
        def _(dve):
            dve.wait_ge(w_in, 64)
            dve.wait_ge(consts, 7)
            dve.tensor_scalar(att_cols[:, 0:HEADS], head_mask[:, :], att[:, 0:1], None, ALU.mult)
            dve.tensor_scalar(att_cols[:, HEADS:8], head_mask[:, :], att[:, 1:2], None, ALU.mult).then_inc(w_ready, 1)
            dve.wait_ge(wt_psum, 1)
            dve.tensor_copy(w_ext[:, 0:HF], ps[:, 0, 0:P]).then_inc(w_ready, 1)
            dve.wait_ge(wt_psum, 2)
            dve.tensor_copy(w_ext[:, HF:HF + 8], ps[:, 1, 0:8]).then_inc(w_ready, 1)
            for c in range(STEPS):
                bank, half = 4 * (c % 2), c % 2
                dve.wait_ge(xT_psum, c + 1)
                if c >= 2:
                    dve.wait_ge(proj_psum, c - 1)
                dve.tensor_copy(xT[:, half, :], ps[:, bank, :]).then_inc(xT_sbuf, 1)
                if c % 4 == 3 and c > 3:
                    largest(dve, c // 4 - 1)
            largest(dve, 3)
            dve.wait_ge(sd_copied, STEPS)
            dve.tensor_copy(d_cols[:, :, :], sd[:, :, HEADS:8].rearrange("p t h -> p h t")).then_inc(d_turn, 1)
            dve.wait_ge(tile_maxed, RING)
            dve.tensor_reduce(part_max[:, 0:HEADS], tile_max[:, :, :].rearrange("p t h -> p h t"), AX.X,
                              ALU.max).then_inc(prep, 1)
            dve.tensor_reduce(part_max[:, HEADS:8], sd[:, :, 0:HEADS].rearrange("p t h -> p h t"), AX.X,
                              ALU.max).then_inc(prep, 1)
            dve.wait_ge(d_turn, 2)
            dve.tensor_copy(dT[:, :, :], ps[:, 3, 0:2 * P].rearrange("p (k n) -> p k n", k=2)).then_inc(d_turn, 2)
            dve.wait_ge(max_psum, 1)
            dve.tensor_reduce(row_max[:, :], ps[0:8, 0, 0:P], AX.X, ALU.max).then_inc(prep, 1)
            dve.wait_ge(prep, 3)
            dve.tensor_scalar(diag_max[:, :], ident[0:8, 0:8], row_max[:, 0:1], None, ALU.mult).then_inc(prep, 1)
            dve.tensor_scalar(s_neg[:, :, :], sd[:, :, 0:HEADS], -1.0, None, ALU.mult)
            dve.tensor_scalar(s_steep[:, :, :], sd[:, :, 0:HEADS], STEEP, None, ALU.mult)
            dve.wait_ge(max_psum, 2)
            dve.tensor_copy(glob[:, :], ps[:, 4, 0:8]).then_inc(prep, 1)
            dve.wait_ge(prep, 5)
            largest_s = glob[:, HEADS:8].rearrange("p (a h) -> p a h", a=1).to_broadcast([P, NT, HEADS])
            dve.tensor_tensor(s_rel[:, :, :], sd[:, :, 0:HEADS], largest_s, ALU.subtract).then_inc(prep, 1)
            dve.tensor_tensor(d_rel[:, :, :], sd[:, :, HEADS:8], largest_s, ALU.add).then_inc(prep, 1)
            dve.tensor_scalar(head_size[:, :], glob[:, 0:HEADS], 1e-30, None, ALU.max).then_inc(prep, 1)
            dve.wait_ge(prep, 8)
            dve.reciprocal(inv_size[:, :], head_size[:, :]).then_inc(prep, 1)
            dve.wait_ge(exps, 2)
            dve.tensor_scalar(wgt[:, :, :, :], wgt[:, :, :, :], FEATURE_SCALE, None, ALU.mult).then_inc(prep, 1)
            dve.wait_ge(prep, 10)
            dve.tensor_tensor(wgt_n[:, :, :, :].rearrange("p q t h -> p (q t) h"),
                              wgt[:, :, :, :].rearrange("p q t h -> p (q t) h"),
                              inv_size[:, :].rearrange("p (a h) -> p a h", a=1).to_broadcast([P, 2 * NT, HEADS]),
                              ALU.mult).then_inc(wgt_ready, 1)
            dve.wait_ge(wgt_ready, 1)
            for n in range(GP_FROM + 1):
                if n < GP_FROM:
                    if n >= 3:
                        dve.wait_ge(feat_step, feat_at(f"R{n - 3}"))
                    multiply(dve, n).then_inc(val_ready["v"], 1)
                if n >= 1:
                    dve.wait_ge(val_ready["v"], n)
                    dve.wait_ge(feat_step, feat_at(f"H{n - 1}"))
                    subtract_high(dve, n - 1).then_inc(val_rest["v"], 1)
            for part in range(2):
                dve.tensor_copy(feat[:, :, :, part * HALF + FO], wgt[:, part, :, :]).then_inc(den_done, 1)
                dve.wait_ge(den_done, 3 * part + 1)
                dve.tensor_tensor(wgt[:, part, :, :], wgt[:, part, :, :], feat[:, :, :, part * HALF + FO],
                                  ALU.subtract).then_inc(den_done, 1)
                dve.wait_ge(den_done, 3 * part + 2)
                dve.tensor_scalar(feat[:, :, :, part * HALF + V + FO], wgt[:, part, :, :], REST_SCALE, None,
                                  ALU.mult).then_inc(den_done, 1)

            dve.sem_inc(psum_free, TPB)

            def masks_of(b, parity, g, of=None):
                slot = g % RING
                dve.wait_ge(slot_free, b * NG + (g + 1))
                if g == 0:
                    dve.wait_ge(d_in[parity], (b - parity) * 8 + 16)
                share = ACT_SHARE[g % len(ACT_SHARE)]
                for n in range(share, JG * HEADS):
                    if of is not None and n - share < TPB:
                        add_rest(of, n - share)
                    j, h = n // HEADS, n % HEADS
                    jt = g * JG + j
                    op = dve.tensor_scalar(m_u8[:, slot, j, :, h], d_v[:, parity, h, :], s_neg[:, jt, h:h + 1], ONE8,
                                           ALU.is_gt, ALU.mult)
                op.then_inc(cmp_v, 1)
                if g == NG - 1:
                    dve.wait_ge(cmp_v, b * NG + NG)
                    dve.sem_inc(d_used_v, 1)
                dve.wait_ge(cmp_v, b * NG + (g + 1))
                dve.wait_ge(cmp_s, b * NG + (g + 1))
                dve.wait_ge(adj_in[slot], b * (16 * NG // RING) + 16 * (g // RING + 1))
                dve.tensor_tensor(masks[:, slot, :], masks[:, slot, :], adj_f[:, slot, :], ALU.min).then_inc(masks_ready, 1)

            EPI = 5

            def add_rest(b, t):
                dve.wait_ge(rest_copied, b * TPB + (t + 1))
                for bank in range(2):
                    op = dve.tensor_tensor(sums[:, t, 6 * bank:6 * bank + 6, :],
                                           ps[:, 2 * t + bank, 0:12 * V].rearrange("p (q l v) -> p q l v", l=2, v=V)[:, :, 0, :],
                                           rest[:, t, 6 * bank:6 * bank + 6, :], ALU.add)
                op.then_inc(psum_free, 1)

            def attention(b):
                dve.wait_ge(psum_free, b * TPB + 2 * TPB)
                for t in range(TPB):
                    op = dve.scalar_tensor_tensor(out=tail_part[:, t, :, :], in0=sums[:, t, 8:12, :], scalar=1.0 / ADJ8,
                                                  in1=by_part[:, t, :, 1, :], op0=ALU.mult, op1=ALU.subtract)
                op.then_inc(epi, 1)
                dve.tensor_tensor(main_part[:, :, :, :], by_part[:, :, :, 0, :],
                                  q_all[:, bass.ds(b * TPB, TPB), :].rearrange("p t (h o) -> p t h o", o=1)
                                  .to_broadcast([P, TPB, HEADS, V]), ALU.mult).then_inc(epi, 1)
                dve.wait_ge(epi, b * EPI + 2)
                dve.tensor_tensor(main_part[:, :, :, :], main_part[:, :, :, :], tail_part[:, :, :, :], ALU.add).then_inc(epi, 1)
                dve.wait_ge(epi, b * EPI + 3)
                dve.reciprocal(inv_den[:, :, :], main_part[:, :, :, FO]).then_inc(epi, 1)
                dve.wait_ge(epi, b * EPI + 4)
                dve.tensor_tensor(inv_den[:, :, :], inv_den[:, :, :],
                                  head_size[:, :].rearrange("p (a h) -> p a h", a=1).to_broadcast([P, TPB, HEADS]),
                                  ALU.mult).then_inc(epi, 1)
                dve.wait_ge(epi, b * EPI + 5)
                dve.tensor_tensor(y[:, :, :].rearrange("p t (h f) -> p t h f", h=HEADS), main_part[:, :, :, 0:FO],
                                  inv_den[:, :, :].rearrange("p t (h o) -> p t h o", o=1)
                                  .to_broadcast([P, TPB, HEADS, FO]), ALU.mult).then_inc(y_ready, 1)

            def residual_stats(b):
                dve.wait_ge(y_ready, b * 3 + 1)
                dve.wait_ge(xb_ready, b + 1)
                dve.tensor_tensor(y[:, :, :], y[:, :, :], xb[:, :, :], ALU.add).then_inc(y_ready, 1)
                dve.wait_ge(y_ready, b * 3 + 2)
                for t in range(TPB):
                    op = dve.bn_stats(stats[:, t, :], y[:, t, :])
                op.then_inc(y_ready, 1)
                dve.wait_ge(y_ready, b * 3 + 3)
                dve.nop(nofuse=True)
                for t in range(TPB):
                    op = dve.bn_aggr(mean_var[:, t, :], stats[:, t, :])
                op.then_inc(mv_ready, 1)

            def normalise(b, first=False):
                dve.wait_ge(rstd_step, b * 2 + 2)
                if not first:
                    dve.wait_ge(stored, b * 16)
                for t in range(TPB):
                    op = dve.tensor_scalar(y_out[:, t, :], y[:, t, :], mean_var[:, t, 0:1], rstd[:, t:t + 1],
                                           ALU.subtract, ALU.mult)
                op.then_inc(norm_done, 1)

            def rotated(b, parity, first=False, last=False):
                for g in range(AHEAD, NG):
                    masks_of(b, parity, g)
                if last:
                    for t in range(TPB):
                        add_rest(b, t)
                    attention(b)
                    residual_stats(b)
                    normalise(b)
                    return
                for g in range(AHEAD):
                    masks_of(b + 1, 1 - parity, g, of=b if g == EVAC_GROUP else None)
                    if g == EVAC_GROUP:
                        attention(b)
                    if g == EVAC_GROUP + 1:
                        residual_stats(b)
                    if g == EVAC_GROUP + 2:
                        normalise(b, first)

            for g in range(AHEAD):
                masks_of(0, 0, g)
            rotated(0, 0, first=True)
            rotated(1, 1)
            with dve.Fori(1, NB // 2 - 1) as pair:
                rotated(pair * 2, 0)
                rotated(pair * 2 + 1, 1)
            rotated(NB - 2, 0)
            rotated(NB - 1, 1, last=True)


_INS = ["x", "adj", "L0_gnn_weight", "L0_gnn_att_src", "L0_gnn_att_dst", "L0_gnn_bias"]


def kernel(**inputs):
    import numpy as np
    import concourse.bacc as bacc
    from concourse.bass_utils import run_bass_kernel_spmd

    nc = bacc.Bacc("TRN2", target_bir_lowering=False, num_devices=1)
    arrays, args = {}, []
    for name in _INS:
        a = np.ascontiguousarray(inputs[name])
        arrays[f"in_{name}"] = a
        args.append(nc.dram_tensor(f"in_{name}", a.shape, mybir.dt.from_np(a.dtype), kind="ExternalInput").ap())
    out = nc.dram_tensor("out_x", arrays["in_x"].shape, F32, kind="ExternalOutput").ap()
    gat_resnorm(nc, *args, out)
    r = run_bass_kernel_spmd(nc, [arrays], core_ids=[0])
    return r.results[0]["out_x"]
```

```python
from contextlib import ExitStack

import concourse.bass as bass
from concourse import mybir

ALU = mybir.AluOpType
ACT = mybir.ActivationFunctionType
AX = mybir.AxisListType
F32 = mybir.dt.float32
F16 = mybir.dt.float16
F8 = mybir.dt.float8e4
U8 = mybir.dt.uint8

P = 128
ONE8 = 56.0
ADJ8 = 1.875
STEEP = 2.0 ** 30
FEATURE_SCALE = 2.0 ** 13
REST_SCALE = 2.0 ** 11
LEAK = 0.2
EPS = 1e-5

JG = 2
RING = 8
ROUND = 2
QUARTERS = 4
TPB = 4
IB = TPB * P
ACT_SHARE = (5, 4, 5, 4, 5, 4, 5, 4, 5, 4, 5, 4, 5, 4, 4, 4)
AHEAD = 13
EVAC = {5: (0, 1), 6: (2, 3)}
EPILOGUE = (7, 10, 12)


def gat_resnorm(nc, x, adj, weight, att_src, att_dst, bias, out):
    N, K = x.shape
    HEADS, FO = att_src.shape[1], att_src.shape[2]
    HF = HEADS * FO
    NT = N // P
    NB = N // IB
    NG = NT // JG
    V = FO + 1
    SPAN = 4 * V
    HALF = 2 * V
    assert K == P and HF == P and N % IB == 0 and NT % JG == 0 and NG % RING == 0 and NG % ROUND == 0
    assert NB % 2 == 0 and 3 * SPAN <= 512 and NT // TPB == NB
    assert all(2 * len(tiles) <= min(ACT_SHARE[g], JG * HEADS - ACT_SHARE[g]) + 1 for g, tiles in EVAC.items())
    assert AHEAD > max(EPILOGUE) and AHEAD >= RING and RING % ROUND == 0
    CH = NT // QUARTERS
    STEPS = NT // 4

    dT_dram = nc.dram_tensor("dT_scratch", (HEADS, N), F32).ap()

    with ExitStack() as ctx:
        def sb(name, shape, dt=F32):
            return ctx.enter_context(nc.sbuf_tensor(name, shape, dt))

        def sem(name):
            return ctx.enter_context(nc.semaphore(name))

        ps = ctx.enter_context(nc.psum_tensor("ps", [P, 8, 512], F32))

        feat = sb("feat", [P, NT, HEADS, SPAN], F16)
        adj_f = sb("adj_f", [P, RING, JG * IB])
        masks = sb("masks", [P, RING, JG * IB])
        d_rows = sb("d_rows", [P, 2, HEADS * IB])
        s_neg = sb("s_neg", [P, NT, HEADS])
        s_steep = sb("s_steep", [P, NT, HEADS])
        q_all = sb("q_all", [P, NT, HEADS])
        head_size = sb("head_size", [P, HEADS])
        work = sb("work", [P, 2, TPB * 12 * V])
        tail_part = sb("tail_part", [P, TPB, HEADS, V])
        main_part = sb("main_part", [P, TPB, HEADS, V])
        inv_den = sb("inv_den", [P, TPB, HEADS])
        xb = sb("xb", [P, TPB, HF])
        y = sb("y", [P, TPB, HF])
        y_out = sb("y_out", [P, TPB, HF])
        stats = sb("stats", [P, TPB, 6])
        mean_var = sb("mean_var", [P, TPB, 2])
        var_eps = sb("var_eps", [P, TPB])
        rstd = sb("rstd", [P, TPB])
        minus_half = sb("minus_half", [P, TPB])
        bias_rows = sb("bias_rows", [P, HF])
        ident = sb("ident", [P, P])
        ones = sb("ones", [8, P])
        w_nat = sb("w_nat", [P, K])
        att = sb("att", [P, 2])
        head_mask = sb("head_mask", [P, HEADS])
        att_cols = sb("att_cols", [P, 8])
        w_ext = sb("w_ext", [P, HF + 8])
        xT = sb("xT", [P, 2, 512])
        d_cols = sb("d_cols", [P, HEADS, NT])
        dT = sb("dT", [P, 2, P])
        tile_max = sb("tile_max", [P, NT, HEADS])
        sd = sb("sd", [P, NT, 8])
        part_max = sb("part_max", [P, 8])
        row_max = sb("row_max", [8, 1])
        diag_max = sb("diag_max", [8, 8])
        glob = sb("glob", [P, 8])
        inv_size = sb("inv_size", [P, HEADS])
        s_rel = sb("s_rel", [P, NT, HEADS])
        d_rel = sb("d_rel", [P, NT, HEADS])
        wgt = sb("wgt", [P, 2, NT, HEADS])
        wgt_n = sb("wgt_n", [P, 2, NT, HEADS])
        val = sb("val", [P, 2, CH * HF])

        vals = {"v": (val[:, 0, :], val[:, 1, :]),
                "g": (work[:, :, :].rearrange("p w n -> p (w n)")[:, 0:CH * HF], d_rows[:, 1, :])}
        rest = work[:, 0, :].rearrange("p (t q v) -> p t q v", t=TPB, v=V)
        sums = work[:, 1, :].rearrange("p (t q v) -> p t q v", t=TPB, v=V)
        xs = adj_f[:, :, :].rearrange("p r (t k) -> p (r t) k", k=K)
        hp = masks[:, :, :].rearrange("p r (t k) -> p (r t) k", k=HF)
        adj_v = adj_f[:, :, :].rearrange("p r (j n) -> p r j n", j=JG)
        m_u8 = masks[:, :, :].bitcast(U8).rearrange("p r (j n h) -> p r j n h", j=JG, h=HEADS)
        m_f8 = masks[:, :, :].bitcast(F8).rearrange("p r (j n h) -> p r j n h", j=JG, h=HEADS)
        a_f8 = adj_f[:, :, :].bitcast(F8).rearrange("p r (j n h) -> p r j n h", j=JG, h=4)
        d_v = d_rows[:, :, :].rearrange("p b (h n) -> p b h n", h=HEADS)
        by_part = sums[:, :, 0:8, :].rearrange("p t (h q) v -> p t h q v", q=2)

        w_in = sem("w_in")
        bias_in = sem("bias_in")
        x_in = [sem(f"x_in{r}") for r in range(QUARTERS)]
        consts = sem("consts")
        wt_psum = sem("wt_psum")
        w_ready = sem("w_ready")
        xT_psum = sem("xT_psum")
        xT_sbuf = sem("xT_sbuf")
        proj_psum = sem("proj_psum")
        h_copied = sem("h_copied")
        sd_copied = sem("sd_copied")
        d_turn = sem("d_turn")
        dT_out = sem("dT_out")
        tile_maxed = sem("tile_maxed")
        prep = sem("prep")
        max_psum = sem("max_psum")
        exps = sem("exps")
        wgt_ready = sem("wgt_ready")
        val_ready = {"v": sem("val_ready_v"), "g": sem("val_ready_g")}
        rounded = sem("rounded")
        rests_made = sem("rests_made")
        left_over = sem("left_over")
        den_done = sem("den_done")
        adj_in = [sem(f"adj_in{r}") for r in range(RING)]
        d_in = [sem("d_in0"), sem("d_in1")]
        d_used_v = sem("d_used_v")
        d_used_s = sem("d_used_s")
        cmp_s = sem("cmp_s")
        cmp_v = sem("cmp_v")
        masks_ready = sem("masks_ready")
        slot_free = sem("slot_free")
        tile_done = sem("tile_done")
        rest_copied = sem("rest_copied")
        psum_free = sem("psum_free")
        epi = sem("epi")
        xb_in = sem("xb_in")
        xb_ready = sem("xb_ready")
        y_ready = sem("y_ready")
        mv_ready = sem("mv_ready")
        rstd_step = sem("rstd_step")
        norm_done = sem("norm_done")
        stored = sem("stored")

        PIECES = 2 * QUARTERS
        GP_FROM = PIECES - 3
        ROUND_ORDER = ("high 0", "high 5", "high 1", "high 6", "high 2", "rest 5", "high 3", "high 4",
                       "rest 6", "high 7", "rest 7")
        ROUND_LATE = {1: 8, 3: 9, 5: 10}
        ROUND_EARLY = len(ROUND_ORDER) - len(ROUND_LATE)

        def piece(n):
            own = vals["v"][n % 2] if n < GP_FROM else vals["g"][(n - GP_FROM) % 2]
            return slice(n // 2 * CH, n // 2 * CH + CH), n % 2, own

        def h_multiplied(eng, g):
            last = 2 * (g * QUARTERS // RING) + 1
            eng.wait_ge(val_ready["v"], min(last + 1, GP_FROM))
            if last >= GP_FROM:
                eng.wait_ge(val_ready["g"], last + 1 - GP_FROM)

        def multiply(eng, n):
            tiles, part, v = piece(n)
            return eng.tensor_tensor(v.rearrange("p (t f) -> p t f", f=FO),
                                     hp[:, tiles, :].rearrange("p t (h f) -> p (t h) f", h=HEADS),
                                     wgt_n[:, part, tiles, :].rearrange("p t (h o) -> p (t h) o", o=1)
                                     .to_broadcast([P, CH * HEADS, FO]), ALU.mult)

        def make_rest(n):
            tiles, part, v = piece(n)
            return nc.vector.scalar_tensor_tensor(out=feat[:, tiles, :, part * HALF + V:part * HALF + V + FO],
                                                  in0=feat[:, tiles, :, part * HALF:part * HALF + FO], scalar=-REST_SCALE,
                                                  in1=v.rearrange("p (t h f) -> p t h f", t=CH, h=HEADS),
                                                  op0=ALU.mult, op1=ALU.add)

        HALVES = (slice(0, TPB // 2), slice(TPB // 2, TPB))

        block = ctx.enter_context(nc.Block())

        @block.sync
        def _(sp):
            sp.dma_start(w_nat[:, :], weight).then_inc(w_in, 16)
            with nc.allow_non_contiguous_dma(reason="two columns of 128 values"):
                sp.dma_start(att[:, 0:1], att_src.rearrange("a h (f o) -> (a h f) o", o=1)).then_inc(w_in, 16)
                sp.dma_start(att[:, 1:2], att_dst.rearrange("a h (f o) -> (a h f) o", o=1)).then_inc(w_in, 16)
            for r in range(QUARTERS):
                sp.dma_start(xs[:, r * CH:(r + 1) * CH, :],
                             x[r * CH * P:(r + 1) * CH * P, :].rearrange("(t p) k -> p t k", p=P)).then_inc(x_in[r], 16)
            sp.dma_start(bias_rows[:, :], bias.rearrange("(a n) -> a n", a=1).to_broadcast([P, HF])).then_inc(bias_in, 16)
            sp.wait_ge(d_turn, 4)
            for k in range(2):
                sp.dma_start(dT_dram.rearrange("h (t p) -> (h t) p", p=P)[k * P:(k + 1) * P, :],
                             dT[:, k, :]).then_inc(dT_out, 16)

            def load_d(b, parity):
                sp.dma_start(d_v[:, parity, :, :],
                             dT_dram[:, bass.ds(b * IB, IB)].rearrange("(a h) n -> a h n", a=1)
                             .to_broadcast([P, HEADS, IB])).then_inc(d_in[parity], 16)

            def load_xb(b):
                sp.dma_start(xb[:, :, :], x[bass.ds(b * IB, IB), :].rearrange("(t p) k -> p t k", p=P)).then_inc(xb_in, 16)

            def store(b, tiles=slice(0, TPB)):
                nodes = bass.ds(b * IB + tiles.start * P, (tiles.stop - tiles.start) * P)
                sp.dma_start(out[nodes, :].rearrange("(t p) k -> p t k", p=P), y_out[:, tiles, :]).then_inc(stored, 16)

            sp.wait_ge(dT_out, 32)
            load_d(0, 0)

            def block_loads(b, parity, first=False, last=False):
                for g in range(NG):
                    r = g % RING
                    if first and g < RING:
                        sp.wait_ge(xT_psum, (g + 1) * STEPS // RING)
                    else:
                        sp.wait_ge(slot_free, b * NG + (g + 1))
                    sp.dma_start(adj_v[:, r, :, :],
                                 adj[g * JG * P:(g + 1) * JG * P, bass.ds(b * IB, IB)]
                                 .rearrange("(j p) n -> p j n", p=P)).then_inc(adj_in[r], 16)
                    if g == NG // 2:
                        if not first:
                            sp.wait_ge(norm_done, b)
                            store(b - 1)
                        load_xb(b)
                        if not last:
                            if first:
                                sp.wait_ge(rounded, len(ROUND_ORDER))
                            else:
                                sp.wait_ge(d_used_v, b)
                                sp.wait_ge(d_used_s, b)
                            load_d(b + 1, 1 - parity)

            block_loads(0, 0, first=True)
            block_loads(1, 1)
            with sp.Fori(1, NB // 2 - 1) as pair:
                block_loads(pair * 2, 0)
                block_loads(pair * 2 + 1, 1)
            block_loads(NB - 2, 0)
            block_loads(NB - 1, 1, last=True)
            for k, tiles in enumerate(HALVES):
                sp.wait_ge(norm_done, NB + k)
                store(NB - 1, tiles)
            sp.wait_ge(stored, 16 * (NB - 1 + len(HALVES)))

        @block.gpsimd
        def _(gp):
            gp.memset(ident[:, :], 0.0).then_inc(consts, 1)
            gp.memset(head_mask[:, :], 0.0).then_inc(consts, 1)
            gp.memset(ones[:, :], 1.0).then_inc(consts, 1)
            gp.memset(minus_half[:, :], -0.5).then_inc(consts, 1)
            gp.wait_ge(consts, 4)
            gp.affine_select(out=ident[:, :], in_=ident[:, :], compare_op=ALU.not_equal, fill=1.0,
                             base=0, pattern=[[-1, P]], channel_multiplier=1).then_inc(consts, 1)
            gp.affine_select(out=head_mask[:, :], in_=head_mask[:, :], compare_op=ALU.is_gt, fill=1.0,
                             base=0, pattern=[[FO, HEADS]], channel_multiplier=-1).then_inc(consts, 1)
            gp.wait_ge(consts, 6)
            gp.affine_select(out=head_mask[:, :], in_=head_mask[:, :], compare_op=ALU.is_gt, fill=0.0,
                             base=FO, pattern=[[FO, HEADS]], channel_multiplier=-1).then_inc(consts, 1)

            def add_bias(b):
                gp.wait_ge(xb_in, b * 16 + 16)
                gp.tensor_tensor(xb[:, :, :], xb[:, :, :],
                                 bias_rows[:, :].rearrange("p (a n) -> p a n", a=1).to_broadcast([P, TPB, HF]),
                                 ALU.add).then_inc(xb_ready, 1)

            def invert_root(k, tiles=slice(0, TPB)):
                gp.wait_ge(mv_ready, k + 1)
                gp.nop(nofuse=True)
                gp.tensor_scalar(var_eps[:, tiles], mean_var[:, tiles, 1], EPS, 1.0, ALU.add, ALU.mult).then_inc(rstd_step, 1)
                gp.wait_ge(rstd_step, k * 2 + 1)
                gp.tensor_tensor(rstd[:, tiles], var_eps[:, tiles], minus_half[:, tiles], ALU.pow).then_inc(rstd_step, 1)

            gp.wait_ge(wgt_ready, 4)
            for n in range(GP_FROM, PIECES + 1):
                if n < PIECES:
                    if n >= GP_FROM + 2:
                        gp.wait_ge(rounded, ROUND_ORDER.index(f"rest {n - 2}") + 1)
                    multiply(gp, n).then_inc(val_ready["g"], 1)
                if n > GP_FROM:
                    gp.wait_ge(val_ready["g"], n - GP_FROM)
                    gp.wait_ge(rounded, ROUND_ORDER.index(f"high {n - 1}") + 1)
                    tiles, part, v = piece(n - 1)
                    v = v.rearrange("p (t h f) -> p t h f", t=CH, h=HEADS)
                    gp.tensor_tensor(v, v, feat[:, tiles, :, part * HALF:part * HALF + FO], ALU.subtract).then_inc(left_over, 1)

            gp.wait_ge(bias_in, 16)
            with gp.Fori(0, NB - 1) as b:
                add_bias(b)
                invert_root(b)
            add_bias(NB - 1)
            for k, tiles in enumerate(HALVES):
                invert_root(NB - 1 + k, tiles)

        @block.tensor
        def _(pe):
            pe.wait_ge(w_in, 48)
            pe.wait_ge(consts, 5)
            pe.transpose(ps[:, 0, 0:P], w_nat[:, :], ident[:, :]).then_inc(wt_psum, 1)
            pe.wait_ge(w_ready, 1)
            pe.matmul(ps[:, 1, 0:8], w_nat[:, :], att_cols[:, :], start=True, stop=True).then_inc(wt_psum, 1)
            pe.wait_ge(w_ready, 3)

            def turn(c):
                bank = 4 * (c % 2)
                if c % 4 == 0:
                    pe.wait_ge(x_in[c // 4], 16)
                if c >= 2:
                    pe.wait_ge(xT_sbuf, c - 1)
                for t in range(4):
                    mm = pe.transpose(ps[:, bank, t * P:(t + 1) * P], xs[:, 4 * c + t, :], ident[:, :])
                mm.then_inc(xT_psum, 1)

            turn(0)
            for c in range(STEPS):
                if c + 1 < STEPS:
                    turn(c + 1)
                bank, half = 4 * (c % 2), c % 2
                pe.wait_ge(xT_sbuf, c + 1)
                if c >= 2:
                    pe.wait_ge(h_copied, c - 1)
                    pe.wait_ge(sd_copied, c - 1)
                for t in range(4):
                    mm = pe.matmul(ps[:, bank + 1 + t // 3, t % 3 * (HF + 8):(t % 3 + 1) * (HF + 8)],
                                   xT[:, half, t * P:(t + 1) * P], w_ext[:, :], start=True, stop=True)
                mm.then_inc(proj_psum, 1)

            pe.wait_ge(d_turn, 1)
            for k in range(2):
                mm = pe.transpose(ps[:, 3, k * P:(k + 1) * P],
                                  d_cols[:, :, :].rearrange("p h t -> p (h t)")[:, k * P:(k + 1) * P], ident[:, :])
            mm.then_inc(d_turn, 1)

            pe.wait_ge(prep, 2)
            pe.transpose(ps[0:8, 0, 0:P], part_max[:, :], ident[:, :]).then_inc(max_psum, 1)
            pe.wait_ge(prep, 4)
            pe.matmul(ps[:, 4, 0:8], ones[:, :], diag_max[:, :], start=True, stop=True).then_inc(max_psum, 1)

            pe.sem_inc(slot_free, RING - 1)
            pe.sem_inc(tile_done, 1)
            pe.wait_ge(prep, 5)
            pe.wait_ge(d_turn, 4)
            pe.wait_ge(den_done, 6)

            def features_made(q):
                last = 2 * q + 1
                pe.wait_ge(rests_made, min(last + 1, GP_FROM))
                if last >= GP_FROM:
                    pe.wait_ge(rounded, ROUND_ORDER.index(f"rest {last}") + 1)

            with pe.Fori(0, NB) as b:
                for rnd in range(NG // ROUND):
                    if rnd * QUARTERS % (NG // ROUND) == 0:
                        features_made(rnd * QUARTERS // (NG // ROUND))
                    for t in range(TPB):
                        if rnd == 0:
                            pe.wait_ge(psum_free, b * TPB + (t + 1))
                            pe.nop(nofuse=True)
                        cols = slice(t * P, (t + 1) * P)
                        for j in range(ROUND * JG):
                            g = rnd * ROUND + j // JG
                            jt, slot, js = g * JG + j % JG, g % RING, j % JG
                            if t == 0 and j == 0:
                                pe.wait_ge(masks_ready, b * (NG // ROUND) + (rnd + 1))
                                pe.nop(nofuse=True)
                            first, last = jt == 0, jt == NT - 1
                            for h in range(3):
                                pe.matmul(ps[:, 2 * t, h * SPAN:(h + 1) * SPAN], m_f8[:, slot, js, cols, h],
                                          feat[:, jt, h, :], start=first and h == 0, stop=last and h == 2,
                                          skip_group_check=True)
                            pe.matmul(ps[:, 2 * t + 1, 0:SPAN], m_f8[:, slot, js, cols, 3],
                                      feat[:, jt, 3, :], start=first, stop=False, skip_group_check=True)
                            mm = pe.matmul(ps[:, 2 * t + 1, SPAN:SPAN + HEADS * HALF], a_f8[:, slot, js, cols, 3],
                                           feat[:, jt, :, HALF:SPAN], start=False, stop=last, skip_group_check=True)
                            if last:
                                mm.then_inc(tile_done, 1)
                            elif t == TPB - 1 and js == JG - 1:
                                mm.then_inc(slot_free, 1)
                        if rnd == 0 and t == 0:
                            pe.wait_ge(tile_done, b * TPB + 1)
                            pe.sem_inc(slot_free, 1)

        @block.scalar
        def _(act):
            for c in range(STEPS):
                bank = 4 * (c % 2)
                act.wait_ge(proj_psum, c + 1)
                for t, n in ((0, 3), (3, 1)):
                    from_psum = ps[:, bank + 1 + t // 3, 0:n * (HF + 8)].rearrange("p (t k) -> p t k", t=n)
                    tiles = slice(4 * c + t, 4 * c + t + n)
                    op_h = act.activation(hp[:, tiles, :], from_psum[:, :, 0:HF], ACT.Copy)
                    if t:
                        op_h.then_inc(h_copied, 1)
                    op_sd = act.activation(sd[:, tiles, :], from_psum[:, :, HF:HF + 8], ACT.Copy)
                    if t:
                        op_sd.then_inc(sd_copied, 1)
            act.wait_ge(prep, 6)
            act.activation(wgt[:, 0, :, :], s_rel[:, :, :], ACT.Exp).then_inc(exps, 1)
            act.activation(wgt[:, 1, :, :], s_rel[:, :, :], ACT.Exp, scale=LEAK).then_inc(exps, 1)
            act.wait_ge(prep, 7)
            act.activation(q_all[:, :, :], d_rel[:, :, :], ACT.Exp, scale=1.0 - LEAK).then_inc(exps, 1)
            act.preload_act_table(ACT.Sigmoid)

            def round_part(step):
                kind, n = step.split()[0], int(step.split()[1])
                tiles, part, v = piece(n)
                v = v.rearrange("p (t h f) -> p t h f", t=CH, h=HEADS)
                maker, count = ("v", n + 1) if n < GP_FROM else ("g", n - GP_FROM + 1)
                if kind == "high":
                    act.wait_ge(val_ready[maker], count)
                    act.activation(feat[:, tiles, :, part * HALF:part * HALF + FO], v, ACT.Copy,
                                   scale=1.0 / REST_SCALE if maker == "v" else 1.0).then_inc(rounded, 1)
                else:
                    act.wait_ge(left_over, count)
                    act.activation(feat[:, tiles, :, part * HALF + V:part * HALF + V + FO], v, ACT.Copy,
                                   scale=REST_SCALE).then_inc(rounded, 1)

            for step in ROUND_ORDER[:ROUND_EARLY]:
                round_part(step)

            def compare(b, parity, g, of=None):
                slot = g % RING
                act.wait_ge(slot_free, b * NG + (g + 1))
                if g == 0:
                    act.wait_ge(d_in[parity], (b - parity) * 8 + 16)
                act.nop(nofuse=True)
                tiles = EVAC.get(g, ()) if of is not None else ()
                for n in range(ACT_SHARE[g % len(ACT_SHARE)]):
                    if n % 2 == 0 and n // 2 < len(tiles):
                        copy_rest(of, tiles[n // 2])
                    j, h = n // HEADS, n % HEADS
                    jt = g * JG + j
                    op = act.activation(m_f8[:, slot, j, :, h], d_v[:, parity, h, :], ACT.Sigmoid,
                                        scale=STEEP, bias=s_steep[:, jt, h:h + 1], saturate=False)
                op.then_inc(cmp_s, 1)
                if g == NG - 1:
                    act.wait_ge(cmp_s, b * NG + NG)
                    act.sem_inc(d_used_s, 1)

            def copy_rest(b, t):
                act.wait_ge(tile_done, b * TPB + (t + 2))
                if t == 0:
                    act.wait_ge(psum_free, b * TPB + TPB)
                for bank in range(2):
                    op = act.activation(rest[:, t, 6 * bank:6 * bank + 6, :],
                                        ps[:, 2 * t + bank, 0:12 * V].rearrange("p (q l v) -> p q l v", l=2, v=V)[:, :, 1, :],
                                        ACT.Copy, scale=1.0 / REST_SCALE)
                op.then_inc(rest_copied, 1)

            def rotated(b, parity, last=False):
                for g in range(AHEAD, NG):
                    compare(b, parity, g)
                if last:
                    for t in range(TPB):
                        copy_rest(b, t)
                else:
                    for g in range(AHEAD):
                        compare(b + 1, 1 - parity, g, of=b)

            for g in range(AHEAD):
                if g < RING:
                    h_multiplied(act, g)
                compare(0, 0, g)
                if g in ROUND_LATE:
                    round_part(ROUND_ORDER[ROUND_LATE[g]])
            with act.Fori(0, NB // 2 - 1) as pair:
                rotated(pair * 2, 0)
                rotated(pair * 2 + 1, 1)
            rotated(NB - 2, 0)
            rotated(NB - 1, 1, last=True)

        def largest(dve, first_step, steps):
            dve.wait_ge(h_copied, first_step + steps)
            tiles = slice(4 * first_step, 4 * (first_step + steps))
            dve.tensor_reduce(tile_max[:, tiles, :].rearrange("p t h -> p (t h)"),
                              hp[:, tiles, :].rearrange("p t (h f) -> p (t h) f", h=HEADS), AX.X, ALU.max,
                              apply_absolute_value=True).then_inc(tile_maxed, steps)

        @block.vector
        def _(dve):
            dve.wait_ge(w_in, 48)
            dve.wait_ge(consts, 7)
            dve.tensor_scalar(att_cols[:, 0:HEADS], head_mask[:, :], att[:, 0:1], None, ALU.mult)
            dve.tensor_scalar(att_cols[:, HEADS:8], head_mask[:, :], att[:, 1:2], None, ALU.mult).then_inc(w_ready, 1)
            dve.wait_ge(wt_psum, 1)
            dve.tensor_copy(w_ext[:, 0:HF], ps[:, 0, 0:P]).then_inc(w_ready, 1)
            dve.wait_ge(wt_psum, 2)
            dve.tensor_copy(w_ext[:, HF:HF + 8], ps[:, 1, 0:8]).then_inc(w_ready, 1)
            for c in range(STEPS):
                bank, half = 4 * (c % 2), c % 2
                dve.wait_ge(xT_psum, c + 1)
                if c >= 2:
                    dve.wait_ge(proj_psum, c - 1)
                dve.tensor_copy(xT[:, half, :], ps[:, bank, :]).then_inc(xT_sbuf, 1)
                if c % 2 == 1 and c > 1:
                    largest(dve, c - 3, 2)
            largest(dve, STEPS - 2, 2)
            dve.wait_ge(sd_copied, STEPS)
            dve.tensor_copy(d_cols[:, :, :], sd[:, :, HEADS:8].rearrange("p t h -> p h t")).then_inc(d_turn, 1)
            dve.wait_ge(tile_maxed, STEPS)
            dve.tensor_reduce(part_max[:, 0:HEADS], tile_max[:, :, :].rearrange("p t h -> p h t"), AX.X,
                              ALU.max).then_inc(prep, 1)
            dve.tensor_reduce(part_max[:, HEADS:8], sd[:, :, 0:HEADS].rearrange("p t h -> p h t"), AX.X,
                              ALU.max).then_inc(prep, 1)
            dve.wait_ge(d_turn, 2)
            dve.tensor_copy(dT[:, :, :], ps[:, 3, 0:2 * P].rearrange("p (k n) -> p k n", k=2)).then_inc(d_turn, 2)
            dve.wait_ge(max_psum, 1)
            dve.tensor_reduce(row_max[:, :], ps[0:8, 0, 0:P], AX.X, ALU.max).then_inc(prep, 1)
            dve.wait_ge(prep, 3)
            dve.tensor_scalar(diag_max[:, :], ident[0:8, 0:8], row_max[:, 0:1], None, ALU.mult).then_inc(prep, 1)
            dve.tensor_scalar(s_neg[:, :, :], sd[:, :, 0:HEADS], -1.0, None, ALU.mult)
            dve.tensor_scalar(s_steep[:, :, :], sd[:, :, 0:HEADS], STEEP, None, ALU.mult)
            dve.wait_ge(max_psum, 2)
            dve.tensor_copy(glob[:, :], ps[:, 4, 0:8]).then_inc(prep, 1)
            dve.wait_ge(prep, 5)
            largest_s = glob[:, HEADS:8].rearrange("p (a h) -> p a h", a=1).to_broadcast([P, NT, HEADS])
            dve.tensor_tensor(s_rel[:, :, :], sd[:, :, 0:HEADS], largest_s, ALU.subtract).then_inc(prep, 1)
            dve.tensor_tensor(d_rel[:, :, :], sd[:, :, HEADS:8], largest_s, ALU.add).then_inc(prep, 1)
            dve.tensor_scalar(head_size[:, :], glob[:, 0:HEADS], 1e-30, None, ALU.max).then_inc(prep, 1)
            dve.wait_ge(prep, 8)
            dve.reciprocal(inv_size[:, :], head_size[:, :]).then_inc(prep, 1)
            dve.wait_ge(exps, 2)
            dve.wait_ge(prep, 9)
            for part in range(2):
                own = (GP_FROM + 1 - part) // 2 * CH
                for tiles, scale in ((slice(0, own), FEATURE_SCALE * REST_SCALE), (slice(own, NT), FEATURE_SCALE)):
                    dve.scalar_tensor_tensor(out=wgt_n[:, part, tiles, :], in0=wgt[:, part, tiles, :], scalar=scale,
                                             in1=inv_size[:, :].rearrange("p (a h) -> p a h", a=1)
                                             .to_broadcast([P, tiles.stop - tiles.start, HEADS]),
                                             op0=ALU.mult, op1=ALU.mult).then_inc(wgt_ready, 1)
            dve.wait_ge(wgt_ready, 4)
            for n in range(GP_FROM + 1):
                if n < GP_FROM:
                    if n >= 2:
                        dve.wait_ge(rests_made, n - 1)
                    multiply(dve, n).then_inc(val_ready["v"], 1)
                if n >= 1:
                    dve.wait_ge(val_ready["v"], n)
                    dve.wait_ge(rounded, ROUND_ORDER.index(f"high {n - 1}") + 1)
                    make_rest(n - 1).then_inc(rests_made, 1)
            dve.tensor_scalar(wgt[:, :, :, :], wgt[:, :, :, :], FEATURE_SCALE, None, ALU.mult).then_inc(prep, 1)
            dve.wait_ge(prep, 10)
            for part in range(2):
                dve.tensor_copy(feat[:, :, :, part * HALF + FO], wgt[:, part, :, :]).then_inc(den_done, 1)
                dve.wait_ge(den_done, 3 * part + 1)
                dve.tensor_tensor(wgt[:, part, :, :], wgt[:, part, :, :], feat[:, :, :, part * HALF + FO],
                                  ALU.subtract).then_inc(den_done, 1)
                dve.wait_ge(den_done, 3 * part + 2)
                dve.tensor_scalar(feat[:, :, :, part * HALF + V + FO], wgt[:, part, :, :], REST_SCALE, None,
                                  ALU.mult).then_inc(den_done, 1)

            dve.sem_inc(psum_free, TPB)

            def compare(b, parity, g, of=None, before=None):
                slot = g % RING
                dve.wait_ge(slot_free, b * NG + (g + 1))
                if g == 0:
                    dve.wait_ge(d_in[parity], (b - parity) * 8 + 16)
                tiles = EVAC.get(g, ()) if of is not None else ()
                share = ACT_SHARE[g % len(ACT_SHARE)]
                for n in range(share, JG * HEADS):
                    if (n - share) % 2 == 0 and (n - share) // 2 < len(tiles):
                        add_rest(of, tiles[(n - share) // 2])
                    j, h = n // HEADS, n % HEADS
                    jt = g * JG + j
                    op = dve.tensor_scalar(m_u8[:, slot, j, :, h], d_v[:, parity, h, :], s_neg[:, jt, h:h + 1], ONE8,
                                           ALU.is_gt, ALU.mult)
                op.then_inc(cmp_v, 1)
                if g == NG - 1:
                    dve.wait_ge(cmp_v, b * NG + NG)
                    dve.sem_inc(d_used_v, 1)
                if before is not None and before[1] % ROUND == ROUND - 1:
                    keep_edges(*before)

            def keep_edges(b, g):
                slots = slice(g % RING - (ROUND - 1), g % RING + 1)
                dve.wait_ge(cmp_v, b * NG + (g + 1))
                dve.wait_ge(cmp_s, b * NG + (g + 1))
                for slot in range(g % RING - (ROUND - 1), g % RING + 1):
                    dve.wait_ge(adj_in[slot], b * (16 * NG // RING) + 16 * (g // RING + 1))
                dve.tensor_tensor(masks[:, slots, :], masks[:, slots, :], adj_f[:, slots, :], ALU.min).then_inc(masks_ready, 1)

            EPI = 5

            def add_rest(b, t):
                dve.wait_ge(rest_copied, b * TPB + (t + 1))
                for bank in range(2):
                    op = dve.tensor_tensor(sums[:, t, 6 * bank:6 * bank + 6, :],
                                           ps[:, 2 * t + bank, 0:12 * V].rearrange("p (q l v) -> p q l v", l=2, v=V)[:, :, 0, :],
                                           rest[:, t, 6 * bank:6 * bank + 6, :], ALU.add)
                op.then_inc(psum_free, 1)

            def attention(b, k, tiles=slice(0, TPB)):
                n = tiles.stop - tiles.start
                dve.wait_ge(psum_free, b * TPB + (TPB + tiles.stop))
                for t in range(tiles.start, tiles.stop):
                    op = dve.scalar_tensor_tensor(out=tail_part[:, t, :, :], in0=sums[:, t, 8:12, :], scalar=1.0 / ADJ8,
                                                  in1=by_part[:, t, :, 1, :], op0=ALU.mult, op1=ALU.subtract)
                op.then_inc(epi, 1)
                dve.tensor_tensor(main_part[:, tiles, :, :], by_part[:, tiles, :, 0, :],
                                  q_all[:, bass.ds(b * TPB + tiles.start, n), :].rearrange("p t (h o) -> p t h o", o=1)
                                  .to_broadcast([P, n, HEADS, V]), ALU.mult).then_inc(epi, 1)
                dve.wait_ge(epi, k * EPI + 2)
                dve.tensor_tensor(main_part[:, tiles, :, :], main_part[:, tiles, :, :], tail_part[:, tiles, :, :],
                                  ALU.add).then_inc(epi, 1)
                dve.wait_ge(epi, k * EPI + 3)
                dve.reciprocal(inv_den[:, tiles, :], main_part[:, tiles, :, FO]).then_inc(epi, 1)
                dve.wait_ge(epi, k * EPI + 4)
                dve.tensor_tensor(inv_den[:, tiles, :], inv_den[:, tiles, :],
                                  head_size[:, :].rearrange("p (a h) -> p a h", a=1).to_broadcast([P, n, HEADS]),
                                  ALU.mult).then_inc(epi, 1)
                dve.wait_ge(epi, k * EPI + 5)
                dve.tensor_tensor(y[:, tiles, :].rearrange("p t (h f) -> p t h f", h=HEADS), main_part[:, tiles, :, 0:FO],
                                  inv_den[:, tiles, :].rearrange("p t (h o) -> p t h o", o=1)
                                  .to_broadcast([P, n, HEADS, FO]), ALU.mult).then_inc(y_ready, 1)

            def residual_stats(b, k, tiles=slice(0, TPB)):
                dve.wait_ge(xb_ready, b + 1)
                dve.wait_ge(y_ready, k * 3 + 1)
                dve.tensor_tensor(y[:, tiles, :], y[:, tiles, :], xb[:, tiles, :], ALU.add).then_inc(y_ready, 1)
                dve.wait_ge(y_ready, k * 3 + 2)
                for t in range(tiles.start, tiles.stop):
                    op = dve.bn_stats(stats[:, t, :], y[:, t, :])
                op.then_inc(y_ready, 1)
                dve.wait_ge(y_ready, k * 3 + 3)
                dve.nop(nofuse=True)
                for t in range(tiles.start, tiles.stop):
                    op = dve.bn_aggr(mean_var[:, t, :], stats[:, t, :])
                op.then_inc(mv_ready, 1)

            def normalise(b, k, tiles=slice(0, TPB), first=False):
                dve.wait_ge(rstd_step, k * 2 + 2)
                if not first:
                    dve.wait_ge(stored, b * 16)
                for t in range(tiles.start, tiles.stop):
                    op = dve.tensor_scalar(y_out[:, t, :], y[:, t, :], mean_var[:, t, 0:1], rstd[:, t:t + 1],
                                           ALU.subtract, ALU.mult)
                op.then_inc(norm_done, 1)

            def rotated(b, parity, first=False, last=False):
                for g in range(AHEAD, NG):
                    compare(b, parity, g, before=(b, g - 1))
                if last:
                    keep_edges(b, NG - 1)
                    for k, tiles in enumerate(HALVES):
                        for t in range(tiles.start, tiles.stop):
                            add_rest(b, t)
                        attention(b, b + k, tiles)
                        residual_stats(b, b + k, tiles)
                    for k, tiles in enumerate(HALVES):
                        normalise(b, b + k, tiles)
                    return
                for g in range(AHEAD):
                    compare(b + 1, 1 - parity, g, of=b,
                            before=(b + 1, g - 1) if g else (b, NG - 1))
                    if g == EPILOGUE[0]:
                        attention(b, b)
                    if g == EPILOGUE[1]:
                        residual_stats(b, b)
                    if g == EPILOGUE[2]:
                        normalise(b, b, first=first)

            for g in range(AHEAD):
                if g < RING:
                    h_multiplied(dve, g)
                compare(0, 0, g, before=(0, g - 1) if g else None)
            rotated(0, 0, first=True)
            rotated(1, 1)
            with dve.Fori(1, NB // 2 - 1) as pair:
                rotated(pair * 2, 0)
                rotated(pair * 2 + 1, 1)
            rotated(NB - 2, 0)
            rotated(NB - 1, 1, last=True)


_INS = ["x", "adj", "L0_gnn_weight", "L0_gnn_att_src", "L0_gnn_att_dst", "L0_gnn_bias"]


def kernel(**inputs):
    import numpy as np
    import concourse.bacc as bacc
    from concourse.bass_utils import run_bass_kernel_spmd

    nc = bacc.Bacc("TRN2", target_bir_lowering=False, num_devices=1)
    arrays, args = {}, []
    for name in _INS:
        a = np.ascontiguousarray(inputs[name])
        arrays[f"in_{name}"] = a
        args.append(nc.dram_tensor(f"in_{name}", a.shape, mybir.dt.from_np(a.dtype), kind="ExternalInput").ap())
    out = nc.dram_tensor("out_x", arrays["in_x"].shape, F32, kind="ExternalOutput").ap()
    gat_resnorm(nc, *args, out)
    r = run_bass_kernel_spmd(nc, [arrays], core_ids=[0])
    return r.results[0]["out_x"]
```
